# Optimizing a Trainium2 kernel written in Bass

```python
import numpy as np
import jax
import jax.numpy as jnp

def _softmax(x, axis=-1):
    return jax.nn.softmax(x, axis=axis)

def _gelu(x):
    return jax.nn.gelu(x, approximate=True)

def _silu(x):
    return jax.nn.silu(x)

def _sigmoid(x):
    return jax.nn.sigmoid(x)

def _layernorm(x, axis=-1, eps=1e-05):
    m = jnp.mean(x, axis=axis, keepdims=True)
    v = jnp.var(x, axis=axis, keepdims=True)
    return (x - m) / jnp.sqrt(v + eps)

def _scatter_add(tgt, idx, src, axis=0):
    return tgt.at[idx].add(src)

def _segment_sum(src, seg, n):
    return jax.ops.segment_sum(src, seg, n)
kernel_name = 'mk_recurrent_d1_jaxref_r8_f67bcb'

def setup_inputs(seed: int=0):
    np.random.seed(seed)
    _w = jnp.asarray

    def _L0_attn_setup():
        import jax, jax.numpy as jnp
        import numpy as np
        DM, DS, KW, GROUPS = (128, 16, 4, 8)
        BATCH, SEQ = (4, 256)
        EPS = 1e-05

        def _layer_norm(x, g, b):
            mu = jnp.mean(x, axis=-1, keepdims=True)
            var = jnp.var(x, axis=-1, keepdims=True)
            return (x - mu) * jax.lax.rsqrt(var + EPS) * g + b

        def _group_norm(y_bcl, g, b):
            B_, C_, L_ = y_bcl.shape
            yg = y_bcl.reshape(B_, GROUPS, C_ // GROUPS, L_)
            mu = jnp.mean(yg, axis=(2, 3), keepdims=True)
            var = jnp.var(yg, axis=(2, 3), keepdims=True)
            yg = (yg - mu) * jax.lax.rsqrt(var + EPS)
            return yg.reshape(B_, C_, L_) * g[None, :, None] + b[None, :, None]

        def _forward(u, in_proj_w, conv_w, conv_b, out_proj_w, ln_g, ln_b, gn_g, gn_b, A_log, D):
            B_, L_, _ = u.shape
            h = _layer_norm(u, ln_g, ln_b)
            proj = jnp.einsum('bld,od->blo', h, in_proj_w)
            x = proj[..., 0 * DM:1 * DM]
            z = proj[..., 1 * DM:2 * DM]
            dt_raw = proj[..., 2 * DM:3 * DM]
            res = proj[..., 3 * DM:4 * DM]
            Bm = proj[..., 4 * DM:4 * DM + DS]
            Cm = proj[..., 4 * DM + DS:4 * DM + 2 * DS]
            sg = proj[..., 4 * DM + 2 * DS:4 * DM + 3 * DS]
            xc = jax.lax.conv_general_dilated(x.transpose(0, 2, 1), conv_w, window_strides=(1,), padding=[(KW - 1, 0)], feature_group_count=DM, dimension_numbers=('NCH', 'OIH', 'NCH'))
            xc = jax.nn.silu(xc + conv_b[None, :, None]).transpose(0, 2, 1)
            dt = jax.nn.softplus(dt_raw)
            A = -jnp.exp(A_log)

            def step(hstate, t_in):
                dt_t, B_t, C_t, sg_t, x_t = t_in
                dA = jnp.exp(dt_t[..., None] * A)
                hstate = dA * hstate + dt_t[..., None] * B_t[:, None, :] * x_t[..., None]
                y_t = jnp.sum(hstate * C_t[:, None, :], axis=-1)
                s_t = jnp.mean(hstate * jax.nn.sigmoid(sg_t)[:, None, :], axis=1)
                return (hstate, (y_t, s_t))
            tm = lambda a: jnp.swapaxes(a, 0, 1)
            h0 = jnp.zeros((B_, DM, DS), dtype=u.dtype)
            _, (ys, ss) = jax.lax.scan(step, h0, (tm(dt), tm(Bm), tm(Cm), tm(sg), tm(xc)))
            y = tm(ys) + xc * D
            s_seq = tm(ss)
            y = _group_norm(y.transpose(0, 2, 1), gn_g, gn_b).transpose(0, 2, 1)
            y = y * jax.nn.silu(z)
            out = jnp.einsum('blf,of->blo', jnp.concatenate([y, s_seq], axis=-1), out_proj_w)
            return out + res + u
        key = jax.random.key(seed)
        ks = jax.random.split(key, 8)
        proj_dim = 3 * DS + 4 * DM
        A_log = jnp.log(jnp.broadcast_to(jnp.arange(1, DS + 1, dtype=jnp.float32), (DM, DS)))
        return {'u': jax.random.normal(ks[0], (BATCH, SEQ, DM), dtype=jnp.float32), 'in_proj_w': jax.random.normal(ks[1], (proj_dim, DM), dtype=jnp.float32) / np.sqrt(DM), 'conv_w': jax.random.normal(ks[2], (DM, 1, KW), dtype=jnp.float32) / np.sqrt(KW), 'conv_b': jnp.zeros((DM,), dtype=jnp.float32), 'out_proj_w': jax.random.normal(ks[3], (DM, DS + DM), dtype=jnp.float32) / np.sqrt(DS + DM), 'ln_g': jnp.ones((DM,), dtype=jnp.float32), 'ln_b': jnp.zeros((DM,), dtype=jnp.float32), 'gn_g': jnp.ones((DM,), dtype=jnp.float32), 'gn_b': jnp.zeros((DM,), dtype=jnp.float32), 'A_log': A_log, 'D': jnp.ones((DM,), dtype=jnp.float32)}
    _L0_attn_in = _L0_attn_setup()

    def _L0_ffn_setup():
        import jax, jax.numpy as jnp
        import numpy as np
        TOP_K = 2
        key = jax.random.key(seed)
        ks = jax.random.split(key, 8)
        B, S, D = (2, 256, 128)
        N_r, N_s = (16, 2)
        u = jax.random.normal(ks[0], (B, S, D), dtype=jnp.float32)
        centroids = jax.random.normal(ks[1], (N_r, D), dtype=jnp.float32)
        expert_biases = jnp.zeros((N_r,), dtype=jnp.float32)
        Wr = jax.random.normal(ks[2], (N_r, D, D), dtype=jnp.float32) * (1.0 / np.sqrt(D))
        br = jax.random.normal(ks[3], (N_r, D), dtype=jnp.float32) * 0.01
        Ws = jax.random.normal(ks[4], (N_s, D, D), dtype=jnp.float32) * (1.0 / np.sqrt(D))
        bs = jax.random.normal(ks[5], (N_s, D), dtype=jnp.float32) * 0.01
        return {'u': u, 'centroids': centroids, 'expert_biases': expert_biases, 'Wr': Wr, 'br': br, 'Ws': Ws, 'bs': bs}
    _L0_ffn_in = _L0_ffn_setup()
    _d = {'L0_attn_u': _L0_attn_in['u'], 'L0_attn_in_proj_w': _L0_attn_in['in_proj_w'], 'L0_attn_conv_w': _L0_attn_in['conv_w'], 'L0_attn_conv_b': _L0_attn_in['conv_b'], 'L0_attn_out_proj_w': _L0_attn_in['out_proj_w'], 'L0_attn_ln_g': _L0_attn_in['ln_g'], 'L0_attn_ln_b': _L0_attn_in['ln_b'], 'L0_attn_gn_g': _L0_attn_in['gn_g'], 'L0_attn_gn_b': _L0_attn_in['gn_b'], 'L0_attn_A_log': _L0_attn_in['A_log'], 'L0_attn_D': _L0_attn_in['D'], 'L0_ffn_centroids': _L0_ffn_in['centroids'], 'L0_ffn_expert_biases': _L0_ffn_in['expert_biases'], 'L0_ffn_Wr': _L0_ffn_in['Wr'], 'L0_ffn_br': _L0_ffn_in['br'], 'L0_ffn_Ws': _L0_ffn_in['Ws'], 'L0_ffn_bs': _L0_ffn_in['bs']}
    _x0 = _d['L0_attn_u']
    _d['L0_attn_u'] = jax.random.normal(jax.random.fold_in(jax.random.key(seed), 1), (4, 512, 128), dtype=_x0.dtype)
    del _x0
    return _d

def reference(L0_attn_u, L0_attn_in_proj_w, L0_attn_conv_w, L0_attn_conv_b, L0_attn_out_proj_w, L0_attn_ln_g, L0_attn_ln_b, L0_attn_gn_g, L0_attn_gn_b, L0_attn_A_log, L0_attn_D, L0_ffn_centroids, L0_ffn_expert_biases, L0_ffn_Wr, L0_ffn_br, L0_ffn_Ws, L0_ffn_bs):

    def _L0_attn_ref(u, in_proj_w, conv_w, conv_b, out_proj_w, ln_g, ln_b, gn_g, gn_b, A_log, D):
        import jax, jax.numpy as jnp
        import numpy as np
        DM, DS, KW, GROUPS = (128, 16, 4, 8)
        BATCH, SEQ = (4, 256)
        EPS = 1e-05

        def _layer_norm(x, g, b):
            mu = jnp.mean(x, axis=-1, keepdims=True)
            var = jnp.var(x, axis=-1, keepdims=True)
            return (x - mu) * jax.lax.rsqrt(var + EPS) * g + b

        def _group_norm(y_bcl, g, b):
            B_, C_, L_ = y_bcl.shape
            yg = y_bcl.reshape(B_, GROUPS, C_ // GROUPS, L_)
            mu = jnp.mean(yg, axis=(2, 3), keepdims=True)
            var = jnp.var(yg, axis=(2, 3), keepdims=True)
            yg = (yg - mu) * jax.lax.rsqrt(var + EPS)
            return yg.reshape(B_, C_, L_) * g[None, :, None] + b[None, :, None]

        def _forward(u, in_proj_w, conv_w, conv_b, out_proj_w, ln_g, ln_b, gn_g, gn_b, A_log, D):
            B_, L_, _ = u.shape
            h = _layer_norm(u, ln_g, ln_b)
            proj = jnp.einsum('bld,od->blo', h, in_proj_w)
            x = proj[..., 0 * DM:1 * DM]
            z = proj[..., 1 * DM:2 * DM]
            dt_raw = proj[..., 2 * DM:3 * DM]
            res = proj[..., 3 * DM:4 * DM]
            Bm = proj[..., 4 * DM:4 * DM + DS]
            Cm = proj[..., 4 * DM + DS:4 * DM + 2 * DS]
            sg = proj[..., 4 * DM + 2 * DS:4 * DM + 3 * DS]
            xc = jax.lax.conv_general_dilated(x.transpose(0, 2, 1), conv_w, window_strides=(1,), padding=[(KW - 1, 0)], feature_group_count=DM, dimension_numbers=('NCH', 'OIH', 'NCH'))
            xc = jax.nn.silu(xc + conv_b[None, :, None]).transpose(0, 2, 1)
            dt = jax.nn.softplus(dt_raw)
            A = -jnp.exp(A_log)

            def step(hstate, t_in):
                dt_t, B_t, C_t, sg_t, x_t = t_in
                dA = jnp.exp(dt_t[..., None] * A)
                hstate = dA * hstate + dt_t[..., None] * B_t[:, None, :] * x_t[..., None]
                y_t = jnp.sum(hstate * C_t[:, None, :], axis=-1)
                s_t = jnp.mean(hstate * jax.nn.sigmoid(sg_t)[:, None, :], axis=1)
                return (hstate, (y_t, s_t))
            tm = lambda a: jnp.swapaxes(a, 0, 1)
            h0 = jnp.zeros((B_, DM, DS), dtype=u.dtype)
            _, (ys, ss) = jax.lax.scan(step, h0, (tm(dt), tm(Bm), tm(Cm), tm(sg), tm(xc)))
            y = tm(ys) + xc * D
            s_seq = tm(ss)
            y = _group_norm(y.transpose(0, 2, 1), gn_g, gn_b).transpose(0, 2, 1)
            y = y * jax.nn.silu(z)
            out = jnp.einsum('blf,of->blo', jnp.concatenate([y, s_seq], axis=-1), out_proj_w)
            return out + res + u
        return _forward(u, in_proj_w, conv_w, conv_b, out_proj_w, ln_g, ln_b, gn_g, gn_b, A_log, D)

    def _L0_ffn_ref(u, centroids, expert_biases, Wr, br, Ws, bs):
        import jax, jax.numpy as jnp
        import numpy as np
        TOP_K = 2
        N_r = centroids.shape[0]
        N_s = Ws.shape[0]
        raw_scores = jnp.einsum('bsd,ed->bse', u, centroids)
        s = jax.nn.softmax(raw_scores + expert_biases, axis=-1)
        topk_vals, topk_idx = jax.lax.top_k(s, TOP_K)
        g_topk = jnp.sum(jax.nn.one_hot(topk_idx, N_r, dtype=s.dtype) * topk_vals[..., None], axis=-2)
        xe = jnp.einsum('bsd,eod->bseo', u, Wr) + br
        routed = jnp.einsum('bse,bseo->bso', g_topk, xe)
        shared = (jnp.einsum('bsd,eod->bso', u, Ws) + jnp.sum(bs, axis=0)) / N_s
        return u + routed + shared
    x = L0_attn_u
    xn = _layernorm(x, axis=-1)
    s = _L0_attn_ref(xn, L0_attn_in_proj_w, L0_attn_conv_w, L0_attn_conv_b, L0_attn_out_proj_w, L0_attn_ln_g, L0_attn_ln_b, L0_attn_gn_g, L0_attn_gn_b, L0_attn_A_log, L0_attn_D)
    g = _silu(_L0_ffn_ref(xn, L0_ffn_centroids, L0_ffn_expert_biases, L0_ffn_Wr, L0_ffn_br, L0_ffn_Ws, L0_ffn_bs))
    x = x + s * g
    return x

_drawn_inputs = setup_inputs


def setup_inputs(seed=0):
    import zlib

    import numpy as np

    out = dict(_drawn_inputs(seed))
    spreads = {'L0_attn_conv_b': (0.0, 0.316),
     'L0_attn_ln_g': (1.0, 0.2),
     'L0_attn_ln_b': (0.0, 0.1),
     'L0_attn_gn_g': (1.0, 0.2),
     'L0_attn_gn_b': (0.0, 0.309),
     'L0_attn_D': (1.0, 0.6),
     'L0_ffn_expert_biases': (0.0, 0.702)}
    factors = {'L0_ffn_br': 8.0, 'L0_ffn_bs': 8.0}
    for name, (base, spread) in spreads.items():
        noise = np.random.default_rng([zlib.crc32(name.encode()), seed]).standard_normal(out[name].shape)
        drawn = base * np.exp(spread * noise) if base else spread * noise
        out[name] = jnp.asarray(drawn.astype(out[name].dtype))
    for name, factor in factors.items():
        out[name] = (out[name] * factor).astype(out[name].dtype)
    return out
```

```python
from contextlib import ExitStack

import numpy as np

import concourse.bass as bass
from concourse import mybir

F32 = mybir.dt.float32
BF16 = mybir.dt.bfloat16
ALU = mybir.AluOpType
ACT = mybir.ActivationFunctionType
AX = mybir.AxisListType.X

B, L, D = 4, 512, 128
DS, KW, GN = 16, 4, 8
E = 16
TT = L // 128
NI = D // DS
NG = D // NI
NQ = 4
SP3 = 3
RING = 2 * NQ
EPS = 1e-5
XP = L + KW - 1

C_ID, C_AVG, C_Y, C_S, C_B, C_G, C_END = np.cumsum([0, 128, 128, NQ * 32, 32, NQ * NI, E]).tolist()
W_DT, W_X, W_Z, W_SG, W_B, W_C, W_CEN, W_END = np.cumsum([0] + [D] * 6 + [E]).tolist()
O_RES, O_Y, O_S, O_END = np.cumsum([0] + [D] * 3).tolist()
(V_CW, V_CB, V_LG, V_LB, V_GG, V_GB, V_D, V_BS, V_A, V_EB, V_END) = np.cumsum(
    [0, KW, 1, 1, 1, 1, 1, 1, 2, NG, E]).tolist()


def mamba_moe(nc, x, xT, const, vec, w_in, w_out, w_r, w_s, b_r, out):
    with ExitStack() as ctx:
        def sb(name, shape, dt=F32):
            return ctx.enter_context(nc.sbuf_tensor(name, shape, dt))

        def pb(name):
            return ctx.enter_context(nc.psum_tensor(name, [128, L], F32))

        def sem(name):
            return ctx.enter_context(nc.semaphore(name))

        cst = sb("cst", [128, C_END])
        vecs = sb("vecs", [128, V_END])
        win = sb("win", [128, W_END])
        wout = sb("wout", [128, O_END])
        wr = sb("wr", [128, E, D])
        ws = sb("ws", [128, 2, D])
        wsum = sb("wsum", [128, D])
        br = sb("br", [E, D])
        ident_b = sb("ident_b", [128, 128], BF16)
        sel_ch = sb("sel_ch", [SP3 * 32, NQ, DS, NI], BF16)
        sel_ex = sb("sel_ex", [SP3 * E, E, 128], BF16)
        a_neg = sb("a_neg", [128, NG])
        bias_sh = sb("bias_sh", [128, 1])
        eps_t = sb("eps_t", [128, 1])
        one_t = sb("one_t", [128, 1])
        ident = cst[:, C_ID:C_ID + 128]
        g_avg = cst[:, C_AVG:C_AVG + 128]
        sel_y = cst[:, C_Y:C_Y + NQ * 32].rearrange("p (q m) -> p q m", q=NQ)
        sel_s = cst[:, C_S:C_S + 32]

        def v(i, n=1):
            return vecs[:, i:i + n]

        x_tok = sb("x_tok", [128, B * TT, D])
        x_ch = sb("x_ch", [128, B * L])
        xn_ch = sb("xn_ch", [128, B * L])
        h_ch = sb("h_ch", [128, B * L])
        xpad = sb("xpad", [128, B * XP])
        xc = sb("xc", [128, 2 * L])
        zs = sb("zs", [128, 2 * L])
        sgs = sb("sgs", [128, 2 * L])
        b_row = sb("b_row", [128, 2 * L])
        c_row = sb("c_row", [128, 2 * L])
        g_parts = sb("g_parts", [SP3 * E, 2 * L], BF16)
        g_ch = sb("g_ch", [E, 2 * L])
        dt_parts = sb("dt_parts", [SP3 * 32, NQ, 2 * L], BF16)
        u_parts = sb("u_parts", [SP3 * 32, NQ, 2 * L], BF16)

        st1 = sb("st1", [128, TT, 6]); mv1 = sb("mv1", [128, TT, 2]); r1 = sb("r1", [128, TT])
        st2 = sb("st2", [128, TT, 6]); mv2 = sb("mv2", [128, TT, 2]); r2 = sb("r2", [128, TT])
        xn_tok = sb("xn_tok", [128, TT, D])
        xn_now = sb("xn_now", [128, L])
        xh_tok = sb("xh_tok", [128, TT, D])
        sc = sb("sc", [128, TT, E]); scm = sb("scm", [128, TT, E]); se = sb("se", [128, TT, E])
        mx = sb("mx", [128, TT]); sm = sb("sm", [128, TT]); rs = sb("rs", [128, TT])
        pr = sb("pr", [128, TT, E]); top8 = sb("top8", [128, TT, 8]); top2 = sb("top2", [128, TT, 8])
        rest = sb("rest", [128, TT, E]); gate = sb("gate", [128, TT, E]); gres = sb("gres", [128, TT, E])
        gate3 = sb("gate3", [128, TT, SP3, E], BF16)
        sp = sb("sp", [128, L]); dtv = sb("dtv", [128, L]); uv = sb("uv", [128, L])
        dt3 = sb("dt3", [128, SP3, L], BF16); u3 = sb("u3", [128, SP3, L], BF16)
        dtr = sb("dtr", [128, L]); ur = sb("ur", [128, L])
        cv0 = sb("cv0", [128, L]); cv1 = sb("cv1", [128, L])
        sx_t = sb("sx_t", [128, L]); zl = sb("zl", [128, L]); sz_t = sb("sz_t", [128, L]); sg_t = sb("sg_t", [128, L])
        fv = sb("fv", [128, L]); sf_t = sb("sf_t", [128, L]); gf = sb("gf", [128, L])
        yv = sb("yv", [128, L]); sv = sb("sv", [128, L]); yn = sb("yn", [128, L]); yg = sb("yg", [128, L])
        gst = sb("gst", [128, 6]); gmv = sb("gmv", [128, 2]); gm = sb("gm", [128, 2])
        dm = sb("dm", [128, 1]); dm2 = sb("dm2", [128, 1]); gvar = sb("gvar", [128, 1]); gr = sb("gr", [128, 1])
        ga = sb("ga", [128, 1]); gma = sb("gma", [128, 1]); gc = sb("gc", [128, 1])
        o1 = sb("o1", [128, L]); o2 = sb("o2", [128, L]); o3 = sb("o3", [128, L])
        dbu = sb("dbu", [128, 2, L])
        hs = sb("hs", [128, RING, L])
        hc = sb("hc", [128, RING, L])
        xg = sb("xg", [128, 2, L])

        da_ps = [pb("da_ps0"), pb("da_ps1")]
        u_ps = pb("u_ps")
        g_ps = pb("g_ps")
        f_ps = pb("f_ps")
        y_ps = pb("y_ps")
        s_ps = pb("s_ps")
        work = pb("work")
        work_b = work[:, :].bitcast(BF16)

        sxv, szv, sfv, sgv = sx_t[:, :], sz_t[:, :], sf_t[:, :], sg_t[:, :]

        names = """
        cst_in vec_in win_in wout_in wr_in ws_in br_in x0_in x_in xch_in
        set_dve set_act set_pool consts_ready
        ln1_stats ln1_mv ln1_log ln1_rstd xn_tok_rdy ln2_stats ln2_mv ln2_log ln2_rstd xh_tok_rdy
        pe_xn xn_ch_rdy pe_h h_ch_rdy
        pe_score rt_sc rt_mx rt_scm rt_exp rt_sum rt_rcp rt_pr rt_top rt_top2 rt_rest rt_gate rt_hi rt_res rt_mid rt_lo
        pe_gparts g_parts_rdy pe_gch g_ch_rdy
        pe_dt sp_abs sp_exp sp_ln dtv_rdy pe_x xpad_rdy cv_a cv_b cv_c cv_rdy sx_e sx_l sx_rdy xc_rdy uv_rdy
        dt_hi dt_res dt_mid dt_lo u_hi u_res u_mid u_lo dt_parts_rdy u_parts_rdy
        pe_z zl_rdy sz_e sz_l sz_rdy zs_rdy pe_sg sg_e sg_l sgs_rdy pe_b b_row_rdy pe_c c_row_rdy
        dt_bc da_rdy u_bc dbu_rdy scan_done hc_rdy sums_done
        g_bc xg_rdy ffn_done
        fv_rdy sf_e sf_l sf_rdy gf_rdy yv_rdy sv_rdy gn_stats gn_mv pe_gmu gn_mu gn_dm gn_dm2 pe_gvar gn_var
        gn_log gn_rstd gn_a gn_ma gn_c yn_rdy yg_rdy pe_out o1_rdy o2_rdy o3_rdy out_done
        """.split()
        S = {n: sem(n) for n in names}

        def cols(b):
            return bass.ts(b, L)

        def slot(b):
            return bass.ts(b % 2, L)

        def stepno(b, g):
            return b * NG + (g + 1)

        def ahead(b, g, k):
            return (b, g + k) if g + k < NG else (b + 1, g + k - NG)

        def isfirst(b):
            return isinstance(b, int) and b == 0

        def wait_apart(eng, *pairs):
            pairs = [(name, val if isinstance(val, int) else eng.compute_val(val)) for name, val in pairs]
            eng.wait_ge(S["set_dve"], 1)
            for name, val in pairs:
                eng.wait_ge(S[name], val)

        block = ctx.enter_context(nc.Block())

        @block.sync
        def _(eng):
            eng.dma_start(x_tok[:, 0:TT, :], x[0].rearrange("(t p) d -> p t d", p=128)).then_inc(S["x0_in"], 16)
            eng.dma_start(vecs[:, :], vec).then_inc(S["vec_in"], 16)
            eng.dma_start(cst[:, :], const).then_inc(S["cst_in"], 16)
            eng.dma_start(win[:, :], w_in).then_inc(S["win_in"], 16)
            eng.dma_start(ws[:, :, :], w_s).then_inc(S["ws_in"], 16)
            for b in range(1, B):
                eng.dma_start(x_tok[:, b * TT:(b + 1) * TT, :],
                              x[b].rearrange("(t p) d -> p t d", p=128)).then_inc(S["x_in"], 16)
            eng.dma_start(wr[:, :, :], w_r).then_inc(S["wr_in"], 16)
            eng.dma_start(br[:, :], b_r).then_inc(S["br_in"], 16)
            eng.dma_start(wout[:, :], w_out).then_inc(S["wout_in"], 16)
            eng.dma_start(x_ch[:, :], xT).then_inc(S["xch_in"], 16)

            def stack(n):
                for src, dst, rdy, parts in ((dt3, dt_parts, "dt_parts_rdy", ("dt_hi", "dt_mid", "dt_lo")),
                                             (u3, u_parts, "u_parts_rdy", ("u_hi", "u_mid", "u_lo"))):
                    for s, part in enumerate(parts):
                        wait_apart(eng, (part, n + 1))
                        for j in range(NQ):
                            eng.dma_start(dst[32 * s:32 * s + 32, j, slot(n)],
                                          src[32 * j:32 * j + 32, s, :]).then_inc(S[rdy], 16)

            def store(b):
                wait_apart(eng, ("o3_rdy", b + 1))
                eng.dma_start(out[:, cols(b)], o3[:, :]).then_inc(S["out_done"], 16)

            stack(0)
            stack(1)
            with eng.Fori(1, B - 1) as b:
                store(b - 1)
                stack(b + 1)
            store(B - 2)
            store(B - 1)
            eng.wait_ge(S["out_done"], 16 * B)

        @block.vector
        def _(dve):
            def inc(ins, name):
                ins.then_inc(S[name], 1)

            dve.memset(eps_t[:, :], EPS)
            dve.memset(one_t[:, :], 1.0)
            dve.memset(top2[:, :, :], -1.0)
            inc(dve.memset(xpad[:, :], 0.0), "set_dve")
            dve.wait_ge(S["vec_in"], 16)
            dve.tensor_tensor(bias_sh[:, :], v(V_BS), v(V_BS + 1), ALU.add).then_inc(S["set_dve"], 1)

            def ln1_a(n):
                if isfirst(n):
                    dve.wait_ge(S["x0_in"], 16)
                else:
                    dve.wait_ge(S["x_in"], 16 * (B - 1))
                for t in range(TT):
                    last = dve.bn_stats(st1[:, t, :], x_tok[:, n * TT + t, :])
                inc(last, "ln1_stats")

            def ln1_b(n):
                wait_apart(dve, ("ln1_stats", n + 1))
                for t in range(TT):
                    last = dve.bn_aggr(mv1[:, t, :], st1[:, t, :])
                inc(last, "ln1_mv")

            def ln1_c(n):
                dve.wait_ge(S["ln1_rstd"], n + 1)
                if not isfirst(n):
                    dve.wait_ge(S["pe_h"], n)
                for t in range(TT):
                    last = dve.tensor_scalar(xn_tok[:, t, :], x_tok[:, n * TT + t, :], mv1[:, t, 0:1], r1[:, t:t + 1],
                                             ALU.subtract, ALU.mult)
                inc(last, "xn_tok_rdy")

            def ln2_a(n):
                dve.wait_ge(S["xn_tok_rdy"], n + 1)
                for t in range(TT):
                    last = dve.bn_stats(st2[:, t, :], xn_tok[:, t, :])
                inc(last, "ln2_stats")

            def ln2_b(n):
                wait_apart(dve, ("ln2_stats", n + 1))
                for t in range(TT):
                    last = dve.bn_aggr(mv2[:, t, :], st2[:, t, :])
                inc(last, "ln2_mv")

            def ln2_c(n):
                dve.wait_ge(S["ln2_rstd"], n + 1)
                for t in range(TT):
                    last = dve.tensor_scalar(xh_tok[:, t, :], xn_tok[:, t, :], mv2[:, t, 0:1], r2[:, t:t + 1],
                                             ALU.subtract, ALU.mult)
                inc(last, "xh_tok_rdy")

            def bc_e(t2):
                return t2[:, :].unsqueeze(2).to_broadcast([128, TT, E])

            def rt1(n):
                dve.wait_ge(S["pe_score"], n + 1)
                inc(dve.tensor_tensor(sc[:, :, :], work[:, 0:TT * E].rearrange("p (t e) -> p t e", e=E),
                                      v(V_EB, E).unsqueeze(1).to_broadcast([128, TT, E]), ALU.add), "rt_sc")

            def rt2(n):
                dve.wait_ge(S["rt_sc"], n + 1)
                inc(dve.tensor_reduce(mx[:, :], sc[:, :, :], AX, ALU.max), "rt_mx")

            def rt3(n):
                dve.wait_ge(S["rt_mx"], n + 1)
                inc(dve.tensor_tensor(scm[:, :, :], sc[:, :, :], bc_e(mx), ALU.subtract), "rt_scm")

            def rt4(n):
                dve.wait_ge(S["rt_exp"], n + 1)
                inc(dve.tensor_reduce(sm[:, :], se[:, :, :], AX, ALU.add), "rt_sum")

            def rt5(n):
                dve.wait_ge(S["rt_sum"], n + 1)
                inc(dve.reciprocal(rs[:, :], sm[:, :]), "rt_rcp")

            def rt6(n):
                dve.wait_ge(S["rt_rcp"], n + 1)
                inc(dve.tensor_tensor(pr[:, :, :], se[:, :, :], bc_e(rs), ALU.mult), "rt_pr")

            def rt7(n):
                wait_apart(dve, ("rt_pr", n + 1))
                for t in range(TT):
                    last = dve.max(top8[:, t, :], pr[:, t, :])
                inc(last, "rt_top")

            def rt8(n):
                dve.wait_ge(S["rt_top"], n + 1)
                inc(dve.tensor_copy(top2[:, :, 0:2], top8[:, :, 0:2]), "rt_top2")

            def rt9(n):
                wait_apart(dve, ("rt_top2", n + 1))
                for t in range(TT):
                    last = dve.match_replace(rest[:, t, :], top2[:, t, :], pr[:, t, :], 0.0)
                inc(last, "rt_rest")

            def rt10(n):
                dve.wait_ge(S["rt_rest"], n + 1)
                if not isfirst(n):
                    dve.wait_ge(S["pe_gch"], n)
                inc(dve.tensor_tensor(gate[:, :, :], pr[:, :, :], rest[:, :, :], ALU.subtract), "rt_gate")

            def rt11(n):
                dve.wait_ge(S["rt_gate"], n + 1)
                inc(dve.tensor_copy(gate3[:, :, 0, :], gate[:, :, :]), "rt_hi")

            def rt12(n):
                dve.wait_ge(S["rt_hi"], n + 1)
                inc(dve.tensor_tensor(gres[:, :, :], gate[:, :, :], gate3[:, :, 0, :], ALU.subtract), "rt_res")

            def rt13(n):
                dve.wait_ge(S["rt_res"], n + 1)
                inc(dve.tensor_copy(gate3[:, :, 1, :], gres[:, :, :]), "rt_mid")

            def rt14(n):
                dve.wait_ge(S["rt_mid"], n + 1)
                inc(dve.tensor_tensor(gate3[:, :, 2, :], gres[:, :, :], gate3[:, :, 1, :], ALU.subtract), "rt_lo")

            def softplus(n):
                dve.wait_ge(S["sp_ln"], n + 1)
                if not isfirst(n):
                    dve.wait_ge(S["u_lo"], n)
                inc(dve.scalar_tensor_tensor(dtv[:, :], work[:, :], 0.0, sp[:, :], ALU.max, ALU.add), "dtv_rdy")

            def conv(n, k):
                src = xpad[:, bass.ds(n * XP + k, L)]
                if k == 0:
                    dve.wait_ge(S["xpad_rdy"], n + 1)
                    inc(dve.tensor_scalar(cv0[:, :], src, v(V_CW), v(V_CB), ALU.mult, ALU.add), "cv_a")
                    return
                dve.wait_ge(S[("cv_a", "cv_b", "cv_c")[k - 1]], n + 1)
                if k == 3 and not isfirst(n):
                    dve.wait_ge(S["xc_rdy"], n)
                a, b = (cv0, cv1) if k % 2 else (cv1, cv0)
                inc(dve.scalar_tensor_tensor(b[:, :], src, v(V_CW + k), a[:, :], ALU.mult, ALU.add),
                    ("cv_b", "cv_c", "cv_rdy")[k - 1])

            def inputs(b, g):
                dve.wait_ge(S["u_bc"], stepno(b, g))
                if g == 0:
                    dve.wait_ge(S["b_row_rdy"], b + 1)
                if not (isfirst(b) and g < 2):
                    dve.wait_ge(S["scan_done"], stepno(b, g) - 2)
                inc(dve.tensor_tensor(dbu[:, g % 2, :], u_ps[:, :], b_row[:, slot(b)], ALU.mult), "dbu_rdy")

            def scan(b, g):
                dve.wait_ge(S["da_rdy"], stepno(b, g))
                dve.wait_ge(S["dbu_rdy"], stepno(b, g))
                if not (isfirst(b) and g < RING):
                    dve.wait_ge(S["hc_rdy"], stepno(b, g) - RING)
                    dve.wait_ge(S["sums_done"], b * NQ + g // NQ - 1)
                inc(dve.tensor_tensor_scan(hs[:, g % RING, :], da_ps[g % 2][:, :], dbu[:, g % 2, :], 0.0,
                                           ALU.mult, ALU.add), "scan_done")

            def gated(b, e):
                dve.wait_ge(S["g_bc"], stepno(b, e))
                if not (isfirst(b) and e < 2):
                    dve.wait_ge(S["ffn_done"], stepno(b, e) - 2)
                inc(dve.tensor_tensor(xg[:, e % 2, :], g_ps[:, :], xn_ch[:, cols(b)], ALU.mult), "xg_rdy")

            def ffn_sum(b):
                dve.wait_ge(S["ffn_done"], stepno(b, E - 1))
                dve.wait_ge(S["set_dve"], 3)
                if not isfirst(b):
                    dve.wait_ge(S["gf_rdy"], b)
                inc(dve.scalar_tensor_tensor(fv[:, :], f_ps[:, :], bias_sh[:, :], xn_ch[:, cols(b)], ALU.add, ALU.add),
                    "fv_rdy")

            def y_sum(b):
                dve.wait_ge(S["sums_done"], NQ * b + NQ)
                dve.wait_ge(S["xc_rdy"], b + 1)
                if not isfirst(b):
                    dve.wait_ge(S["yn_rdy"], b)
                inc(dve.scalar_tensor_tensor(yv[:, :], xc[:, slot(b)], v(V_D), y_ps[:, :], ALU.mult, ALU.add), "yv_rdy")

            def s_sum(b):
                dve.wait_ge(S["sgs_rdy"], b + 1)
                if not isfirst(b):
                    dve.wait_ge(S["pe_out"], b)
                inc(dve.tensor_tensor(sv[:, :], s_ps[:, :], sgs[:, slot(b)], ALU.mult), "sv_rdy")

            def gn1(b):
                dve.wait_ge(S["yv_rdy"], b + 1)
                inc(dve.bn_stats(gst[:, :], yv[:, :]), "gn_stats")

            def gn2(b):
                wait_apart(dve, ("gn_stats", b + 1))
                inc(dve.bn_aggr(gmv[:, :], gst[:, :]), "gn_mv")

            def gn3(b):
                dve.wait_ge(S["pe_gmu"], b + 1)
                inc(dve.tensor_copy(gm[:, :], work[:, 0:2]), "gn_mu")

            def gn4(b):
                dve.wait_ge(S["gn_mu"], b + 1)
                inc(dve.tensor_tensor(dm[:, :], gmv[:, 0:1], gm[:, 0:1], ALU.subtract), "gn_dm")
                dve.wait_ge(S["gn_dm"], b + 1)
                inc(dve.tensor_tensor(dm2[:, :], dm[:, :], dm[:, :], ALU.mult), "gn_dm2")

            def gn5(b):
                dve.wait_ge(S["pe_gvar"], b + 1)
                inc(dve.tensor_tensor(gvar[:, :], work[:, 0:1], gm[:, 1:2], ALU.add), "gn_var")

            def gn6(b):
                dve.wait_ge(S["gn_rstd"], b + 1)
                inc(dve.tensor_tensor(ga[:, :], gr[:, :], v(V_GG), ALU.mult), "gn_a")
                dve.wait_ge(S["gn_a"], b + 1)
                inc(dve.tensor_tensor(gma[:, :], gm[:, 0:1], ga[:, :], ALU.mult), "gn_ma")
                dve.wait_ge(S["gn_ma"], b + 1)
                inc(dve.tensor_tensor(gc[:, :], v(V_GB), gma[:, :], ALU.subtract), "gn_c")

            def plus_u(b):
                dve.wait_ge(S["pe_out"], b + 1)
                if not isfirst(b):
                    dve.wait_ge(S["o2_rdy"], b)
                inc(dve.tensor_tensor(o1[:, :], work[:, :], xn_ch[:, cols(b)], ALU.add), "o1_rdy")

            def sequence(b, before, after):
                n = b + 1
                for g in range(NG):
                    if g < NG - 1 or after:
                        inputs(*ahead(b, g, 1))
                    if before:
                        if g == 0:
                            ffn_sum(b - 1)
                        if g == 3:
                            gn2(b - 1)
                        if g == 4:
                            gn3(b - 1)
                        if g == 5:
                            gn5(b - 1)
                        if g == 6:
                            gn6(b - 1)
                        if g == 9:
                            plus_u(b - 1)
                    if after:
                        if g == 1:
                            ln1_b(n)
                        if g == 2:
                            ln2_a(n)
                        if g == 6:
                            softplus(n)
                        if g == 7:
                            conv(n, 0)
                        if g == 8:
                            conv(n, 3)
                        if g == 9:
                            rt3(n)
                        if g == 10:
                            rt6(n)
                        if g == 11:
                            rt9(n)
                        if g == 12:
                            rt12(n)
                    scan(b, g)
                    if before:
                        if g == 2:
                            y_sum(b - 1)
                            s_sum(b - 1)
                        if g == 4:
                            gn4(b - 1)
                    if after:
                        if g == 0:
                            ln1_a(n)
                        if g == 2:
                            ln2_b(n)
                        if g == 7:
                            conv(n, 1)
                        if g == 8:
                            rt1(n)
                        if g == 10:
                            rt7(n)
                        if g == 11:
                            rt10(n)
                        if g == 12:
                            rt13(n)
                    gated(b, g)
                    if before and g == 2:
                        gn1(b - 1)
                    if after:
                        if g == 1:
                            ln1_c(n)
                        if g == 3:
                            ln2_c(n)
                        if g == 7:
                            conv(n, 2)
                        if g == 8:
                            rt2(n)
                        if g == 9:
                            rt4(n)
                            rt5(n)
                        if g == 10:
                            rt8(n)
                        if g == 11:
                            rt11(n)
                        if g == 12:
                            rt14(n)

            ln1_a(0)
            ln1_b(0)
            dve.wait_ge(S["cst_in"], 16)
            dve.tensor_copy(sel_ch[:, :, :, :], cst[0:SP3 * 32, C_B:C_B + NQ * NI].rearrange(
                "p (q i) -> p q i", q=NQ).unsqueeze(2).to_broadcast([SP3 * 32, NQ, DS, NI]))
            dve.tensor_copy(ident_b[:, :], ident).then_inc(S["consts_ready"], 1)
            ln1_c(0)
            ln2_a(0)
            ln2_b(0)
            ln2_c(0)
            dve.tensor_copy(sel_ex[:, :, :], cst[0:SP3 * E, C_G:C_G + E].unsqueeze(2).to_broadcast(
                [SP3 * E, E, 128])).then_inc(S["consts_ready"], 1)
            dve.wait_ge(S["ws_in"], 16)
            dve.tensor_tensor(wsum[:, :], ws[:, 0, :], ws[:, 1, :], ALU.add).then_inc(S["set_dve"], 1)
            dve.wait_ge(S["set_dve"], 3)
            dve.tensor_scalar(wsum[:, :], wsum[:, :], 0.5, None, ALU.mult).then_inc(S["consts_ready"], 1)
            dve.tensor_scalar(bias_sh[:, :], bias_sh[:, :], 0.5, None, ALU.mult).then_inc(S["set_dve"], 1)
            softplus(0)
            for k in range(KW):
                conv(0, k)
            for rt in (rt1, rt2, rt3, rt4, rt5, rt6, rt7, rt8, rt9, rt10, rt11, rt12, rt13, rt14):
                rt(0)

            inputs(0, 0)
            sequence(0, False, True)
            with dve.Fori(1, B - 1) as b:
                sequence(b, True, True)
            sequence(B - 1, True, False)
            b = B - 1
            for piece in (ffn_sum, y_sum, s_sum, gn1, gn2, gn3, gn4, gn5, gn6, plus_u):
                piece(b)

        @block.scalar
        def _(act):
            def go(name, dst, src, func, **kw):
                act.activation(dst, src, func, **kw).then_inc(S[name], 1)

            def sigmoid(part, n, names, t, src):
                if part == 0:
                    go(names[0], t, src, ACT.Exp, scale=-1.0)
                elif part == 1:
                    act.wait_ge(S[names[0]], n + 1)
                    go(names[1], t, t, ACT.Ln, bias=one_t[:, :])
                else:
                    act.wait_ge(S[names[1]], n + 1)
                    go(names[2], src, t, ACT.Exp, scale=-1.0)

            def rstd(n, need, mid, done, var, t):
                act.wait_ge(S[need], n + 1)
                go(mid, t, var, ACT.Ln, bias=eps_t[:, :])
                act.wait_ge(S[mid], n + 1)
                go(done, t, t, ACT.Exp, scale=-0.5)

            def xn_out(n):
                act.wait_ge(S["pe_xn"], n + 1)
                act.activation(xn_now[:, :], work[:, :], ACT.Copy)
                go("xn_ch_rdy", xn_ch[:, cols(n)], work[:, :], ACT.Copy)

            def h_out(n):
                act.wait_ge(S["pe_h"], n + 1)
                go("h_ch_rdy", h_ch[:, cols(n)], work[:, :], ACT.Identity, scale=v(V_LG), bias=v(V_LB))

            def sp_1(n):
                act.wait_ge(S["pe_dt"], n + 1)
                go("sp_abs", sp[:, :], work[:, :], ACT.Abs)

            def sp_2(n):
                act.wait_ge(S["sp_abs"], n + 1)
                go("sp_exp", sp[:, :], sp[:, :], ACT.Exp, scale=-1.0)

            def sp_3(n):
                act.wait_ge(S["sp_exp"], n + 1)
                go("sp_ln", sp[:, :], sp[:, :], ACT.Ln, bias=one_t[:, :])

            def x_out(n):
                act.wait_ge(S["pe_x"], n + 1)
                act.wait_ge(S["set_dve"], 1)
                go("xpad_rdy", xpad[:, bass.ds(n * XP + KW - 1, L)], work[:, :], ACT.Copy)

            SX = ("sx_e", "sx_l", "sx_rdy")

            def sx(part, n):
                if part == 0:
                    act.wait_ge(S["cv_rdy"], n + 1)
                    if not isfirst(n):
                        act.wait_ge(S["xc_rdy"], n)
                sigmoid(part, n, SX, sxv, cv1[:, :] if part == 0 else sxv)

            def zl_out(n):
                act.wait_ge(S["pe_z"], n + 1)
                if not isfirst(n):
                    act.wait_ge(S["zs_rdy"], n)
                go("zl_rdy", zl[:, :], work[:, :], ACT.Copy)

            def szp(part, n):
                if part == 0:
                    act.wait_ge(S["zl_rdy"], n + 1)
                sigmoid(part, n, ("sz_e", "sz_l", "sz_rdy"), szv, zl[:, :] if part == 0 else szv)

            def sgp(part, n):
                if part == 0:
                    act.wait_ge(S["pe_sg"], n + 1)
                sigmoid(part, n, ("sg_e", "sg_l", "sgs_rdy"), sgv, work[:, :] if part == 0 else sgs[:, slot(n)])

            def sfp(part, b):
                if part == 0:
                    act.wait_ge(S["fv_rdy"], b + 1)
                    if not isfirst(b):
                        act.wait_ge(S["gf_rdy"], b)
                sigmoid(part, b, ("sf_e", "sf_l", "sf_rdy"), sfv, fv[:, :] if part == 0 else sfv)

            def row_out(n, pe, rdy, dst):
                act.wait_ge(S[pe], n + 1)
                go(rdy, dst[:, slot(n)], work[:, :], ACT.Copy)

            def part_hi(n, need, done, src, dst, moved):
                act.wait_ge(S[need], n + 1)
                if not isfirst(n):
                    act.wait_ge(S[moved], 16 * NQ * SP3 * n)
                go(done, dst[:, 0, :], src[:, :], ACT.Copy)

            def part_mid(n, need, done, src, dst):
                act.wait_ge(S[need], n + 1)
                go(done, dst[:, 1, :], src[:, :], ACT.Copy)

            def rt_exp(n):
                act.wait_ge(S["rt_scm"], n + 1)
                go("rt_exp", se[:, :, :], scm[:, :, :], ACT.Exp)

            def g_parts_out(n):
                act.wait_ge(S["pe_gparts"], n + 1)
                go("g_parts_rdy", g_parts[:, slot(n)], work_b[0:SP3 * E, 0:L], ACT.Copy)

            def g_ch_out(n):
                act.wait_ge(S["pe_gch"], n + 1)
                go("g_ch_rdy", g_ch[:, slot(n)], work[0:E, :], ACT.Copy)

            def decay(b, g):
                act.wait_ge(S["dt_bc"], stepno(b, g))
                go("da_rdy", da_ps[g % 2][:, :], da_ps[g % 2][:, :], ACT.Exp, scale=a_neg[:, g:g + 1])

            def gn_apply(b):
                act.wait_ge(S["gn_c"], b + 1)
                act.wait_ge(S["yv_rdy"], b + 1)
                if not isfirst(b):
                    act.wait_ge(S["yg_rdy"], b)
                go("yn_rdy", yn[:, :], yv[:, :], ACT.Identity, scale=ga[:, :], bias=gc[:, :])

            def hi_dt(n):
                part_hi(n, "dtv_rdy", "dt_hi", dtv, dt3, "dt_parts_rdy")

            def hi_u(n):
                part_hi(n, "uv_rdy", "u_hi", uv, u3, "u_parts_rdy")

            def mid_dt(n):
                part_mid(n, "dt_res", "dt_mid", dtr, dt3)

            def mid_u(n):
                part_mid(n, "u_res", "u_mid", ur, u3)

            def ln_rstd(n, k):
                mv, r = ((mv1, r1), (mv2, r2))[k - 1]
                rstd(n, f"ln{k}_mv", f"ln{k}_log", f"ln{k}_rstd", mv[:, :, 1], r[:, :])

            def sequence(b, before, after):
                n = b + 1
                for g in range(NG):
                    if g < NG - 1 or after:
                        decay(*ahead(b, g, 1))
                    if before:
                        if g == 1:
                            sfp(0, b - 1)
                            sfp(1, b - 1)
                        if g == 2:
                            sfp(2, b - 1)
                        if g == 5:
                            rstd(b - 1, "gn_var", "gn_log", "gn_rstd", gvar[:, :], gr[:, :])
                        if g == 6:
                            gn_apply(b - 1)
                    if after:
                        if g == 1:
                            ln_rstd(n, 1)
                        if g == 2:
                            xn_out(n)
                        if g == 3:
                            ln_rstd(n, 2)
                        if g == 4:
                            h_out(n)
                        if g == 5:
                            sp_1(n)
                            sp_2(n)
                            sp_3(n)
                        if g == 6:
                            x_out(n)
                            hi_dt(n)
                        if g == 7:
                            mid_dt(n)
                        if g == 8:
                            sx(0, n)
                            sx(1, n)
                            sx(2, n)
                        if g == 9:
                            rt_exp(n)
                            zl_out(n)
                            szp(0, n)
                        if g == 10:
                            hi_u(n)
                            szp(1, n)
                            sgp(0, n)
                        if g == 11:
                            mid_u(n)
                            szp(2, n)
                            sgp(1, n)
                            row_out(n, "pe_b", "b_row_rdy", b_row)
                        if g == 12:
                            sgp(2, n)
                            row_out(n, "pe_c", "c_row_rdy", c_row)
                        if g == 13:
                            g_parts_out(n)
                        if g == 14:
                            g_ch_out(n)

            act.preload_act_table_set("natural_log_exp_and_others")
            act.wait_ge(S["vec_in"], 16)
            go("set_act", a_neg[:, :], v(V_A, NG), ACT.Exp)
            act.wait_ge(S["set_act"], 1)
            go("set_act", a_neg[:, :], a_neg[:, :], ACT.Copy, scale=-1.0)
            act.wait_ge(S["set_dve"], 1)
            ln_rstd(0, 1)
            ln_rstd(0, 2)
            xn_out(0)
            h_out(0)
            sp_1(0)
            sp_2(0)
            sp_3(0)
            x_out(0)
            hi_dt(0)
            mid_dt(0)
            sx(0, 0)
            sx(1, 0)
            sx(2, 0)
            rt_exp(0)
            row_out(0, "pe_b", "b_row_rdy", b_row)
            hi_u(0)
            row_out(0, "pe_c", "c_row_rdy", c_row)
            mid_u(0)
            zl_out(0)
            szp(0, 0)
            szp(1, 0)
            szp(2, 0)
            sgp(0, 0)
            sgp(1, 0)
            sgp(2, 0)
            g_parts_out(0)
            g_ch_out(0)
            act.wait_ge(S["set_act"], 2)
            decay(0, 0)
            sequence(0, False, True)
            with act.Fori(1, B - 1) as b:
                sequence(b, True, True)
            sequence(B - 1, True, False)
            for part in range(3):
                sfp(part, B - 1)
            rstd(B - 1, "gn_var", "gn_log", "gn_rstd", gvar[:, :], gr[:, :])
            gn_apply(B - 1)

        @block.gpsimd
        def _(pool):
            def tt(name, dst, a, b, op):
                pool.tensor_tensor(dst, a, b, op).then_inc(S[name], 1)

            def outputs(b, g):
                waits = [("scan_done", stepno(b, g))]
                if g == 0:
                    waits.append(("c_row_rdy", b + 1))
                if not (isfirst(b) and g < RING):
                    waits.append(("sums_done", b * NQ + g // NQ - 1))
                wait_apart(pool, *waits)
                tt("hc_rdy", hc[:, g % RING, :], hs[:, g % RING, :], c_row[:, slot(b)], ALU.mult)

            def dt_split(n, k):
                pool.wait_ge(S[("dt_hi", "dt_mid")[k]], n + 1)
                if k == 0:
                    tt("dt_res", dtr[:, :], dtv[:, :], dt3[:, 0, :], ALU.subtract)
                else:
                    tt("dt_lo", dt3[:, 2, :], dtr[:, :], dt3[:, 1, :], ALU.subtract)

            def u_split(n, k):
                pool.wait_ge(S[("u_hi", "u_mid")[k]], n + 1)
                if k == 0:
                    tt("u_res", ur[:, :], uv[:, :], u3[:, 0, :], ALU.subtract)
                else:
                    tt("u_lo", u3[:, 2, :], ur[:, :], u3[:, 1, :], ALU.subtract)

            def x_silu(n):
                wait_apart(pool, ("sx_rdy", n + 1), ("cv_rdy", n + 1))
                tt("xc_rdy", xc[:, slot(n)], cv1[:, :], sxv, ALU.mult)

            def x_dt(n):
                wait_apart(pool, ("xc_rdy", n + 1), ("dtv_rdy", n + 1))
                tt("uv_rdy", uv[:, :], dtv[:, :], xc[:, slot(n)], ALU.mult)

            def z_silu(n):
                wait_apart(pool, ("sz_rdy", n + 1))
                tt("zs_rdy", zs[:, slot(n)], zl[:, :], szv, ALU.mult)

            def f_silu(b):
                pool.wait_ge(S["sf_rdy"], b + 1)
                if not isfirst(b):
                    pool.wait_ge(S["o2_rdy"], b)
                tt("gf_rdy", gf[:, :], fv[:, :], sfv, ALU.mult)

            def y_gate(b):
                wait_apart(pool, ("yn_rdy", b + 1), ("zs_rdy", b + 1),
                           *([] if isfirst(b) else [("pe_out", b)]))
                tt("yg_rdy", yg[:, :], yn[:, :], zs[:, slot(b)], ALU.mult)

            def times_g(b):
                pool.wait_ge(S["o1_rdy"], b + 1)
                pool.wait_ge(S["gf_rdy"], b + 1)
                tt("o2_rdy", o2[:, :], o1[:, :], gf[:, :], ALU.mult)

            def plus_x(b):
                wait_apart(pool, ("o2_rdy", b + 1), ("xch_in", 16),
                           *([] if isfirst(b) else [("out_done", 16 * b)]))
                tt("o3_rdy", o3[:, :], o2[:, :], x_ch[:, cols(b)], ALU.add)

            def sequence(b, before, after):
                n = b + 1
                for g in range(NG):
                    outputs(b, g)
                    if before:
                        if g == 3:
                            f_silu(b - 1)
                        if g == 7:
                            y_gate(b - 1)
                        if g == 11:
                            times_g(b - 1)
                        if g == 13:
                            plus_x(b - 1)
                    if after:
                        if g == 6:
                            dt_split(n, 0)
                        if g == 7:
                            dt_split(n, 1)
                        if g == 8:
                            x_silu(n)
                        if g == 9:
                            x_dt(n)
                        if g == 10:
                            u_split(n, 0)
                        if g == 11:
                            u_split(n, 1)
                        if g == 12:
                            z_silu(n)

            dt_split(0, 0)
            dt_split(0, 1)
            x_silu(0)
            x_dt(0)
            u_split(0, 0)
            u_split(0, 1)
            z_silu(0)
            sequence(0, False, True)
            with pool.Fori(1, B - 1) as b:
                sequence(b, True, True)
            sequence(B - 1, True, False)
            f_silu(B - 1)
            y_gate(B - 1)
            times_g(B - 1)
            plus_x(B - 1)

        @block.tensor
        def _(pe):
            def flip(n, src, rdy, after, done):
                pe.wait_ge(S[rdy], n + 1)
                after()
                for t in range(TT):
                    mm = pe.transpose(work[:, t * 128:(t + 1) * 128], src[:, t, :], ident)
                mm.then_inc(S[done], 1)

            def project(n, w, after, done):
                after()
                pe.matmul(work[:, :], win[:, w:w + D], h_ch[:, cols(n)], start=True, stop=True).then_inc(S[done], 1)

            def last(name, count):
                def wait():
                    pe.wait_ge(S[name], count)
                return wait

            def nothing():
                pass

            def scores(n, after):
                after()
                for t in range(TT):
                    mm = pe.matmul(work[:, t * E:(t + 1) * E], xn_now[:, t * 128:(t + 1) * 128],
                                   win[:, W_CEN:W_CEN + E], start=True, stop=True)
                mm.then_inc(S["pe_score"], 1)

            def gate_parts(n, after):
                wait_apart(pe, ("rt_lo", n + 1))
                after()
                for t in range(TT):
                    mm = pe.transpose(work_b[0:SP3 * E, t * 128:(t + 1) * 128],
                                      gate3[:, t, :, :].rearrange("p s e -> p (s e)"), ident_b[:, :])
                mm.then_inc(S["pe_gparts"], 1)

            def gate_flip(n, after):
                after()
                for t in range(TT):
                    mm = pe.transpose(work[0:E, t * 128:(t + 1) * 128], gate[:, t, :], ident)
                mm.then_inc(S["pe_gch"], 1)

            def spread_dt(b, g):
                if g == 0:
                    pe.wait_ge(S["dt_parts_rdy"], 16 * NQ * SP3 * (b + 1))
                if not (isfirst(b) and g < 2):
                    pe.wait_ge(S["scan_done"], stepno(b, g) - 2)
                q, j = divmod(g, NQ)
                pe.matmul(da_ps[g % 2][:, :], sel_ch[:, q, :, :].rearrange("p n i -> p (n i)"),
                          dt_parts[:, j, slot(b)], start=True, stop=True).then_inc(S["dt_bc"], 1)

            def spread_u(b, g):
                if g == 0:
                    pe.wait_ge(S["u_parts_rdy"], 16 * NQ * SP3 * (b + 1))
                if not (isfirst(b) and g < 1):
                    pe.wait_ge(S["dbu_rdy"], stepno(b, g) - 1)
                q, j = divmod(g, NQ)
                pe.matmul(u_ps[:, :], sel_ch[:, q, :, :].rearrange("p n i -> p (n i)"),
                          u_parts[:, j, slot(b)], start=True, stop=True).then_inc(S["u_bc"], 1)

            def spread_gate(b, e):
                wait_apart(pe, *([("g_parts_rdy", b + 1)] if e == 0 else []),
                           *([] if isfirst(b) and e < 1 else [("xg_rdy", stepno(b, e) - 1)]))
                pe.matmul(g_ps[:, :], sel_ex[:, e, :], g_parts[:, slot(b)], start=True, stop=True).then_inc(S["g_bc"], 1)

            def expert(b, e):
                pe.wait_ge(S["xg_rdy"], stepno(b, e))
                mm = pe.matmul(f_ps[:, :], wr[:, e, :], xg[:, e % 2, :], start=False, stop=(e == E - 1))
                mm.then_inc(S["ffn_done"], 1)

            def shared(b):
                if not isfirst(b):
                    pe.wait_ge(S["fv_rdy"], b)
                else:
                    pe.wait_ge(S["consts_ready"], 3)
                    pe.wait_ge(S["wr_in"], 16)
                    pe.wait_ge(S["br_in"], 16)
                pe.wait_ge(S["g_ch_rdy"], b + 1)
                pe.matmul(f_ps[:, :], wsum[:, :], xn_ch[:, cols(b)], start=True, stop=False)
                pe.matmul(f_ps[:, :], br[:, :], g_ch[:, slot(b)], start=False, stop=False)

            def sums(b, q):
                pe.wait_ge(S["hc_rdy"], b * NG + NQ * (q + 1))
                if q == 0 and not isfirst(b):
                    pe.wait_ge(S["sv_rdy"], b)
                for j in range(NQ):
                    tile = slice(32 * j, 32 * j + 32)
                    pe.matmul(s_ps[tile, :], sel_s, hs[:, (NQ * q + j) % RING, :], start=(q == 0), stop=(q == NQ - 1))
                for j in range(NQ):
                    tile = slice(32 * j, 32 * j + 32)
                    mm = pe.matmul(y_ps[tile, :], sel_y[:, q, :], hc[:, (NQ * q + j) % RING, :],
                                   start=(q == 0), stop=(q == NQ - 1))
                mm.then_inc(S["sums_done"], 1)

            def gn_mean(b, after):
                pe.wait_ge(S["gn_mv"], b + 1)
                after()
                pe.matmul(work[:, 0:2], g_avg, gmv[:, :], start=True, stop=True).then_inc(S["pe_gmu"], 1)

            def gn_spread(b, after):
                pe.wait_ge(S["gn_dm2"], b + 1)
                after()
                pe.matmul(work[:, 0:1], g_avg, dm2[:, :], start=True, stop=True).then_inc(S["pe_gvar"], 1)

            def project_out(b, after):
                after()
                if isfirst(b):
                    pe.wait_ge(S["wout_in"], 16)
                pe.matmul(work[:, :], wout[:, O_RES:O_RES + D], h_ch[:, cols(b)], start=True, stop=False)
                pe.wait_ge(S["sv_rdy"], b + 1)
                pe.matmul(work[:, :], wout[:, O_S:O_S + D], sv[:, :], start=False, stop=False)
                pe.wait_ge(S["yg_rdy"], b + 1)
                pe.matmul(work[:, :], wout[:, O_Y:O_Y + D], yg[:, :], start=False, stop=True).then_inc(S["pe_out"], 1)

            def sequence(b, before, after):
                n = b + 1
                for g in range(NG):
                    if g < NG - 2 or after:
                        spread_u(*ahead(b, g, 2))
                    if before and g == 0:
                        expert(b - 1, E - 1)
                    if before and g == 1:
                        sums(b - 1, NQ - 1)
                    if g == 1:
                        shared(b)
                    if g >= 1:
                        expert(b, g - 1)
                    if g < NG - 2 or after:
                        spread_dt(*ahead(b, g, 2))
                    if g < NG - 1 or after:
                        spread_gate(*ahead(b, g, 1))
                    if g in (5, 9, 13):
                        sums(b, (g - 5) // 4)
                    if after and g == 2:
                        flip(n, xn_tok, "xn_tok_rdy", last("g_ch_rdy", n), "pe_xn")
                    if before and g == 3:
                        gn_mean(b - 1, last("xn_ch_rdy", n + 1) if after else last("g_ch_rdy", n))
                    if after and g == 4:
                        flip(n, xh_tok, "xh_tok_rdy", last("gn_mu", b) if before else last("xn_ch_rdy", n + 1), "pe_h")
                    if before and g == 4:
                        gn_spread(b - 1, last("h_ch_rdy", n + 1) if after else last("gn_mu", b))
                    if after and g == 5:
                        project(n, W_DT, wait_dt(n, b, before), "pe_dt")
                    if after and g == 6:
                        project(n, W_X, last("dtv_rdy", n + 1), "pe_x")
                    if after and g == 7:
                        scores(n, last("xpad_rdy", n + 1))
                    if before and g == 8:
                        project_out(b - 1, last("rt_sc", n + 1) if after else last("gn_var", b))
                    if after and g == 9:
                        project(n, W_Z, last("o1_rdy", b) if before else last("rt_sc", n + 1), "pe_z")
                    if after and g == 10:
                        project(n, W_SG, last("zl_rdy", n + 1), "pe_sg")
                    if after and g == 11:
                        project(n, W_B, last("sg_e", n + 1), "pe_b")
                    if after and g == 12:
                        project(n, W_C, last("b_row_rdy", n + 1), "pe_c")
                    if after and g == 13:
                        gate_parts(n, last("c_row_rdy", n + 1))
                    if after and g == 14:
                        gate_flip(n, last("g_parts_rdy", n + 1))

            def wait_dt(n, b, before):
                def wait():
                    pe.wait_ge(S["h_ch_rdy"], n + 1)
                    if before:
                        pe.wait_ge(S["gn_var"], b)
                return wait

            pe.wait_ge(S["cst_in"], 16)
            flip(0, xn_tok, "xn_tok_rdy", nothing, "pe_xn")
            flip(0, xh_tok, "xh_tok_rdy", last("xn_ch_rdy", 1), "pe_h")
            pe.wait_ge(S["win_in"], 16)
            project(0, W_DT, last("h_ch_rdy", 1), "pe_dt")
            project(0, W_X, last("dtv_rdy", 1), "pe_x")
            scores(0, last("xpad_rdy", 1))
            project(0, W_B, last("rt_sc", 1), "pe_b")
            project(0, W_C, last("b_row_rdy", 1), "pe_c")
            project(0, W_Z, last("c_row_rdy", 1), "pe_z")
            project(0, W_SG, last("zl_rdy", 1), "pe_sg")
            pe.wait_ge(S["consts_ready"], 2)
            gate_parts(0, last("sg_e", 1))
            gate_flip(0, last("g_parts_rdy", 1))
            spread_dt(0, 0)
            spread_u(0, 0)
            spread_gate(0, 0)
            spread_dt(0, 1)
            spread_u(0, 1)
            sequence(0, False, True)
            with pe.Fori(1, B - 1) as b:
                sequence(b, True, True)
            sequence(B - 1, True, False)
            expert(B - 1, E - 1)
            sums(B - 1, NQ - 1)
            gn_mean(B - 1, last("o1_rdy", B - 1))
            gn_spread(B - 1, last("gn_mu", B))
            project_out(B - 1, last("gn_var", B))


def kernel(**inputs):
    import concourse.bacc as bacc
    from concourse.bass_utils import run_bass_kernel_spmd

    a = {k: np.asarray(val) for k, val in inputs.items()}
    x = np.ascontiguousarray(a["L0_attn_u"])

    def f(v):
        return np.asarray(v, np.float32)

    p = np.arange(128)
    const = np.zeros((128, C_END), np.float32)
    const[:, C_ID:C_ID + 128] = np.eye(128)
    const[:, C_AVG:C_AVG + 128] = (p[:, None] // DS == p[None, :] // DS) / (D // GN)
    for q in range(NQ):
        const[p, C_Y + 32 * q + NI * q + p % NI] = 1.0
        for s in range(SP3):
            for i in range(NI):
                const[32 * s + NI * q + i, C_B + NI * q + i] = 1.0
    const[p, C_S + p // NI] = 1.0 / D
    for s in range(SP3):
        const[E * s + np.arange(E), C_G + np.arange(E)] = 1.0

    w = a["L0_attn_in_proj_w"].T
    parts = {name: w[:, lo:hi] for name, lo, hi in (
        ("x", 0, D), ("z", D, 2 * D), ("dt", 2 * D, 3 * D), ("res", 3 * D, 4 * D),
        ("b", 4 * D, 4 * D + DS), ("c", 4 * D + DS, 4 * D + 2 * DS), ("sg", 4 * D + 2 * DS, 4 * D + 3 * DS))}
    sg_tiles = np.zeros((D, NQ, 32), np.float32)
    sg_tiles[:, :, 0:DS] = parts["sg"][:, None, :]
    w_in = np.concatenate([parts["dt"], parts["x"], parts["z"], sg_tiles.reshape(D, D),
                           np.repeat(parts["b"], NI, 1), np.repeat(parts["c"], NI, 1),
                           a["L0_ffn_centroids"].T], 1)
    wo = a["L0_attn_out_proj_w"].T
    wos = np.zeros((NQ, 32, D), np.float32)
    wos[:, 0:DS, :] = wo[None, D:D + DS, :]
    w_out = np.concatenate([parts["res"], wo[0:D], wos.reshape(D, D)], 1)
    a_rows = a["L0_attn_A_log"].reshape(NQ, NQ, NI, DS).transpose(3, 2, 1, 0).reshape(128, NG)
    vec = np.concatenate([
        a["L0_attn_conv_w"][:, 0, :], *[a["L0_attn_" + k][:, None] for k in
                                        ("conv_b", "ln_g", "ln_b", "gn_g", "gn_b", "D")],
        a["L0_ffn_bs"].T, a_rows, np.broadcast_to(a["L0_ffn_expert_biases"], (128, E))], 1)
    arrays = {
        "x": x, "xT": x.reshape(B * L, D).T, "const": const, "vec": vec, "w_in": w_in, "w_out": w_out,
        "w_r": a["L0_ffn_Wr"].transpose(2, 0, 1), "w_s": a["L0_ffn_Ws"].transpose(2, 0, 1), "b_r": a["L0_ffn_br"],
    }
    arrays = {k: np.ascontiguousarray(val) for k, val in arrays.items()}

    nc = bacc.Bacc("TRN2", target_bir_lowering=False, num_devices=1)
    args = [nc.dram_tensor(f"in_{k}", val.shape, mybir.dt.from_np(val.dtype), kind="ExternalInput").ap()
            for k, val in arrays.items()]
    args.append(nc.dram_tensor("out_ch", (D, B * L), F32, kind="ExternalOutput").ap())
    mamba_moe(nc, *args)
    r = run_bass_kernel_spmd(nc, [{f"in_{k}": val for k, val in arrays.items()}], core_ids=[0])
    return np.ascontiguousarray(r.results[0]["out_ch"].T.reshape(B, L, D))
```

```python
from contextlib import ExitStack

import numpy as np

import concourse.bass as bass
from concourse import mybir

F32 = mybir.dt.float32
BF16 = mybir.dt.bfloat16
ALU = mybir.AluOpType
ACT = mybir.ActivationFunctionType
AX = mybir.AxisListType.X

B, L, D = 4, 512, 128
DS, KW, GN = 16, 4, 8
E = 16
TT = L // 128
NI = D // DS
NG = D // NI
NQ = 4
SP3 = 3
RING = 2 * NQ
EPS = 1e-5
XP = L + KW - 1

C_ID, C_AVG, C_Y, C_S, C_B, C_G, C_END = np.cumsum([0, 128, 128, NQ * 32, 32, NQ * NI, E]).tolist()
W_DT, W_X, W_Z, W_SBC, W_CEN, W_END = np.cumsum([0] + [D] * 4 + [E]).tolist()
O_RES, O_Y, O_S, O_END = np.cumsum([0] + [D] * 3).tolist()
(V_CW, V_CB, V_LG, V_LB, V_GG, V_GB, V_D, V_BS, V_A, V_EB, V_END) = np.cumsum(
    [0, KW, 1, 1, 1, 1, 1, 1, 2, NG, E]).tolist()


def mamba_moe(nc, x, xT, const, vec, w_in, w_out, w_r, w_s, b_r, out, dt_moved, u_moved):
    with ExitStack() as ctx:
        def sb(name, shape, dt=F32):
            return ctx.enter_context(nc.sbuf_tensor(name, shape, dt))

        def pb(name):
            return ctx.enter_context(nc.psum_tensor(name, [128, L], F32))

        def sem(name):
            return ctx.enter_context(nc.semaphore(name))

        cst = sb("cst", [128, C_END])
        vecs = sb("vecs", [128, V_END])
        win = sb("win", [128, W_END])
        wout = sb("wout", [128, O_END])
        wr = sb("wr", [128, E, D])
        ws = sb("ws", [128, 2, D])
        wsum = sb("wsum", [128, D])
        br = sb("br", [SP3 * E, D]); br_res = sb("br_res", [SP3 * E, D])
        br_parts = sb("br_parts", [SP3 * E, SP3, D], BF16)
        ident_b = sb("ident_b", [128, 128], BF16)
        sel_ch = sb("sel_ch", [128, NQ, DS, NI], BF16)
        sel_ex = sb("sel_ex", [SP3 * E, E, 128], BF16)
        a_neg = sb("a_neg", [128, NG])
        bias_sh = sb("bias_sh", [128, 1])
        eps_t = sb("eps_t", [128, 1])
        eps2_t = sb("eps2_t", [128, 1])
        one_t = sb("one_t", [128, 1])
        ident = cst[:, C_ID:C_ID + 128]
        g_avg = cst[:, C_AVG:C_AVG + 128]
        sel_y = cst[:, C_Y:C_Y + NQ * 32].rearrange("p (q m) -> p q m", q=NQ)
        sel_s = cst[:, C_S:C_S + 32]

        def v(i, n=1):
            return vecs[:, i:i + n]

        x_tok = sb("x_tok", [128, B * TT, D])
        x_ch = sb("x_ch", [128, B * L])
        xn_ch = sb("xn_ch", [128, B * L])
        h_ch = sb("h_ch", [128, B * L])
        bc_rows = sb("bc_rows", [64, L])
        xpad = sb("xpad", [128, B * XP])
        xc = sb("xc", [128, 2 * L])
        zs = sb("zs", [128, 2 * L])
        sgs = sb("sgs", [128, 2 * L])
        b_row = sb("b_row", [128, 2 * L])
        c_row = sb("c_row", [128, 2 * L])
        g_parts = sb("g_parts", [SP3 * E, 2 * L], BF16)
        dt_parts = sb("dt_parts", [SP3 * 32, NQ, 2 * L], BF16)
        u_parts = sb("u_parts", [SP3 * 32, NQ, 2 * L], BF16)

        st1 = sb("st1", [128, B * TT, 6]); mv1 = sb("mv1", [128, B * TT, 2])
        r1 = sb("r1", [128, B * TT]); r2 = sb("r2", [128, B * TT])
        nm1 = sb("nm1", [128, B * TT]); nm2 = sb("nm2", [128, B * TT])

        xn_tok = sb("xn_tok", [128, TT, D])
        xn_now = sb("xn_now", [128, L])
        xh_tok = sb("xh_tok", [128, TT, D])
        sc = sb("sc", [128, TT, E]); scm = sb("scm", [128, TT, E]); se = sb("se", [128, TT, E])
        mx = sb("mx", [128, TT]); sm = sb("sm", [128, TT]); rs = sb("rs", [128, TT])
        pr = sb("pr", [128, TT, E]); top8 = sb("top8", [128, TT, 8]); top2 = sb("top2", [128, TT, 8])
        rest = sb("rest", [128, TT, E]); gate = sb("gate", [128, TT, E]); gres = sb("gres", [128, TT, E])
        gate3 = sb("gate3", [128, TT, SP3, E], BF16)
        spp = sb("spp", [128, L]); sp = sb("sp", [128, L]); dtv = sb("dtv", [128, L]); uv = sb("uv", [128, L])
        dt3 = sb("dt3", [128, SP3, L], BF16); u3 = sb("u3", [128, SP3, L], BF16)
        dtr = sb("dtr", [128, L]); ur = sb("ur", [128, L])
        cv0 = sb("cv0", [128, L]); cv1 = sb("cv1", [128, L])
        sx_t = sb("sx_t", [128, L]); zl = sb("zl", [128, L]); sz_t = sb("sz_t", [128, L]); sg_t = sb("sg_t", [128, L])
        fv = sb("fv", [128, L]); sf_t = sb("sf_t", [128, L]); gf = sb("gf", [128, L])
        yv = sb("yv", [128, L]); sv = sb("sv", [128, L]); yn = sb("yn", [128, L]); yg = sb("yg", [128, L])
        gst = sb("gst", [128, 6]); gmv = sb("gmv", [128, 2]); gm = sb("gm", [128, 2])
        dm = sb("dm", [128, 1]); dm2 = sb("dm2", [128, 1]); gvar = sb("gvar", [128, 1]); gr = sb("gr", [128, 1])
        ga = sb("ga", [128, 1]); gma = sb("gma", [128, 1]); gc = sb("gc", [128, 1])
        o1 = sb("o1", [128, L]); o2 = sb("o2", [128, L]); o3 = sb("o3", [128, L])
        dbu = sb("dbu", [128, 2, L])
        hs = sb("hs", [128, RING, L])
        hc = sb("hc", [128, RING, L])
        xg = sb("xg", [128, 2, L])

        da_ps = [pb("da_ps0"), pb("da_ps1")]
        u_ps = pb("u_ps")
        g_ps = pb("g_ps")
        f_ps = pb("f_ps")
        y_ps = pb("y_ps")
        s_ps = pb("s_ps")
        work = pb("work")
        work_b = work[:, :].bitcast(BF16)

        sxv, szv, sfv, sgv = sx_t[:, :], sz_t[:, :], sf_t[:, :], sg_t[:, :]

        names = """
        cst_in vec_in win_in wout_in wr_in ws_in br_in x0_in x_in xch_in
        set_dve set_act set_pool consts_ready
        ln_stats ln_mv ln1_log ln1_rstd ln1_shift xn_tok_rdy ln2_log ln2_rstd ln2_shift xh_tok_rdy
        pe_xn xn_ch_rdy pe_h h_ch_rdy
        pe_score rt_sc rt_mx rt_scm rt_exp rt_sum rt_rcp rt_pr rt_top rt_top2 rt_rest rt_gate rt_hi rt_res rt_mid rt_lo
        pe_gparts g_parts_rdy br_hi br_mid br_lo br_left
        pe_dt sp_pos sp_abs sp_exp sp_ln dtv_rdy pe_x xpad_rdy cv_a cv_b cv_c cv_rdy sx_e sx_l sx_rdy xc_rdy uv_rdy
        dt_hi dt_res dt_mid dt_lo u_hi u_res u_mid u_lo dt_parts_out u_parts_out dt_parts_rdy u_parts_rdy
        pe_z zl_rdy sz_e sz_l sz_rdy zs_rdy pe_sg sg_e sg_l sgs_rdy bc_rows_rdy b_row_rdy c_row_rdy
        dt_bc da_rdy u_bc dbu_rdy scan_done hc_rdy sums_done
        g_bc xg_rdy ffn_done
        fv_rdy sf_e sf_l sf_rdy gf_rdy yv_rdy sv_rdy gn_stats gn_mv pe_gmu gn_mu gn_dm gn_dm2 pe_gvar gn_var
        gn_log gn_rstd gn_a gn_ma gn_c yn_rdy yg_rdy pe_out o1_rdy o2_rdy o3_rdy out_done
        """.split()
        S = {n: sem(n) for n in names}

        def cols(b):
            return bass.ts(b, L)

        def slot(b):
            return bass.ts(b % 2, L)

        def stepno(b, g):
            return b * NG + (g + 1)

        def ahead(b, g, k):
            return (b, g + k) if g + k < NG else (b + 1, g + k - NG)

        def isfirst(b):
            return isinstance(b, int) and b == 0

        def wait_apart(eng, *pairs):
            pairs = [(name, val if isinstance(val, int) else eng.compute_val(val)) for name, val in pairs]
            eng.wait_ge(S["set_dve"], 1)
            for name, val in pairs:
                eng.wait_ge(S[name], val)

        block = ctx.enter_context(nc.Block())

        @block.sync
        def _(eng):
            eng.dma_start(x_tok[:, 0:TT, :], x[0].rearrange("(t p) d -> p t d", p=128)).then_inc(S["x0_in"], 16)
            eng.dma_start(vecs[:, :], vec).then_inc(S["vec_in"], 16)
            eng.dma_start(cst[:, :], const).then_inc(S["cst_in"], 16)
            eng.dma_start(win[:, :], w_in).then_inc(S["win_in"], 16)
            eng.dma_start(ws[:, :, :], w_s).then_inc(S["ws_in"], 16)
            for b in range(1, B):
                eng.dma_start(x_tok[:, b * TT:(b + 1) * TT, :],
                              x[b].rearrange("(t p) d -> p t d", p=128)).then_inc(S["x_in"], 16)
            eng.dma_start(wr[:, :, :], w_r).then_inc(S["wr_in"], 16)
            eng.dma_start(br[:, :], b_r).then_inc(S["br_in"], 16)
            eng.dma_start(wout[:, :], w_out).then_inc(S["wout_in"], 16)
            eng.dma_start(x_ch[:, :], xT).then_inc(S["xch_in"], 16)

            def parts_out(n, src, moved, out_rdy, parts):
                for s, part in enumerate(parts):
                    wait_apart(eng, (part, n + 1))
                    eng.dma_start(moved[:, 32 * s:32 * s + 32, cols(n)], src[:, s, :]).then_inc(S[out_rdy], 16)

            def parts_in(n, dst, moved, out_rdy, rdy):
                wait_apart(eng, (out_rdy, 16 * SP3 * (n + 1)))
                eng.dma_start(dst[:, :, slot(n)], moved[:, :, cols(n)].rearrange("j r t -> r j t")).then_inc(S[rdy], 16)

            def bc_spread(n):
                wait_apart(eng, ("bc_rows_rdy", n + 1))
                for dst, lo, rdy in ((b_row, 16, "b_row_rdy"), (c_row, 48, "c_row_rdy")):
                    eng.dma_start(dst[:, slot(n)], bc_rows[lo:lo + DS, :].unsqueeze(1).to_broadcast(
                        [DS, NI, L])).then_inc(S[rdy], 16)

            DT = ("dt_hi", "dt_mid", "dt_lo")
            U = ("u_hi", "u_mid", "u_lo")

            def moves(n):
                if isfirst(n):
                    bc_spread(n)
                parts_out(n, dt3, dt_moved, "dt_parts_out", DT)
                if not isfirst(n):
                    bc_spread(n)
                parts_in(n, dt_parts, dt_moved, "dt_parts_out", "dt_parts_rdy")
                parts_out(n, u3, u_moved, "u_parts_out", U)
                parts_in(n, u_parts, u_moved, "u_parts_out", "u_parts_rdy")

            def store(b):
                wait_apart(eng, ("o3_rdy", b + 1))
                eng.dma_start(out[:, cols(b)], o3[:, :]).then_inc(S["out_done"], 16)

            moves(0)
            moves(1)
            with eng.Fori(1, B - 1) as b:
                moves(b + 1)
                store(b - 1)
            store(B - 2)
            store(B - 1)
            eng.wait_ge(S["out_done"], 16 * B)

        @block.vector
        def _(dve):
            def inc(ins, name):
                ins.then_inc(S[name], 1)

            dve.memset(eps_t[:, :], EPS)
            dve.memset(eps2_t[:, :], EPS * EPS)
            dve.memset(one_t[:, :], 1.0)
            dve.memset(top2[:, :, :], -1.0)
            inc(dve.memset(xpad[:, :], 0.0), "set_dve")
            dve.wait_ge(S["vec_in"], 16)
            dve.tensor_tensor(bias_sh[:, :], v(V_BS), v(V_BS + 1), ALU.add).then_inc(S["set_dve"], 1)

            def ln_stats(k, lo, hi):
                for t in range(lo * TT, hi * TT):
                    last = dve.bn_stats(st1[:, t, :], x_tok[:, t, :])
                inc(last, "ln_stats")
                wait_apart(dve, ("ln_stats", k))
                for t in range(lo * TT, hi * TT):
                    last = dve.bn_aggr(mv1[:, t, :], st1[:, t, :])
                inc(last, "ln_mv")

            def shifts(k, lo, hi):
                tok = slice(lo * TT, hi * TT)
                dve.wait_ge(S["ln_mv"], k)
                for r, nm, rdy, done in ((r1, nm1, "ln1_rstd", "ln1_shift"), (r2, nm2, "ln2_rstd", "ln2_shift")):
                    dve.wait_ge(S[rdy], k)
                    inc(dve.scalar_tensor_tensor(nm[:, tok], mv1[:, tok, 0], -1.0, r[:, tok], ALU.mult, ALU.mult), done)

            def bc_e(t2):
                return t2[:, :].unsqueeze(2).to_broadcast([128, TT, E])

            def rt1(n):
                dve.wait_ge(S["pe_score"], n + 1)
                inc(dve.tensor_tensor(sc[:, :, :], work[:, 0:TT * E].rearrange("p (t e) -> p t e", e=E),
                                      v(V_EB, E).unsqueeze(1).to_broadcast([128, TT, E]), ALU.add), "rt_sc")

            def rt2(n):
                dve.wait_ge(S["rt_sc"], n + 1)
                inc(dve.tensor_reduce(mx[:, :], sc[:, :, :], AX, ALU.max), "rt_mx")

            def rt3(n):
                dve.wait_ge(S["rt_mx"], n + 1)
                inc(dve.tensor_tensor(scm[:, :, :], sc[:, :, :], bc_e(mx), ALU.subtract), "rt_scm")

            def rt4(n):
                dve.wait_ge(S["rt_exp"], n + 1)
                inc(dve.tensor_reduce(sm[:, :], se[:, :, :], AX, ALU.add), "rt_sum")

            def rt5(n):
                dve.wait_ge(S["rt_sum"], n + 1)
                inc(dve.reciprocal(rs[:, :], sm[:, :]), "rt_rcp")

            def rt6(n):
                dve.wait_ge(S["rt_rcp"], n + 1)
                inc(dve.tensor_tensor(pr[:, :, :], se[:, :, :], bc_e(rs), ALU.mult), "rt_pr")

            def rt7(n):
                wait_apart(dve, ("rt_pr", n + 1))
                for t in range(TT):
                    last = dve.max(top8[:, t, :], pr[:, t, :])
                inc(last, "rt_top")

            def rt8(n):
                dve.wait_ge(S["rt_top"], n + 1)
                inc(dve.tensor_copy(top2[:, :, 0:2], top8[:, :, 0:2]), "rt_top2")

            def rt9(n):
                wait_apart(dve, ("rt_top2", n + 1))
                for t in range(TT):
                    last = dve.match_replace(rest[:, t, :], top2[:, t, :], pr[:, t, :], 0.0)
                inc(last, "rt_rest")

            def rt10(n):
                dve.wait_ge(S["rt_rest"], n + 1)
                inc(dve.tensor_tensor(gate[:, :, :], pr[:, :, :], rest[:, :, :], ALU.subtract), "rt_gate")

            def rt11(n):
                dve.wait_ge(S["rt_gate"], n + 1)
                if not isfirst(n):
                    dve.wait_ge(S["pe_gparts"], n)
                inc(dve.tensor_copy(gate3[:, :, 0, :], gate[:, :, :]), "rt_hi")

            def rt12(n):
                dve.wait_ge(S["rt_hi"], n + 1)
                inc(dve.tensor_tensor(gres[:, :, :], gate[:, :, :], gate3[:, :, 0, :], ALU.subtract), "rt_res")

            def rt13(n):
                dve.wait_ge(S["rt_res"], n + 1)
                inc(dve.tensor_copy(gate3[:, :, 1, :], gres[:, :, :]), "rt_mid")

            def rt14(n):
                dve.wait_ge(S["rt_mid"], n + 1)
                inc(dve.tensor_tensor(gate3[:, :, 2, :], gres[:, :, :], gate3[:, :, 1, :], ALU.subtract), "rt_lo")

            def conv(n, k):
                src = xpad[:, bass.ds(n * XP + k, L)]
                dve.wait_ge(S[("cv_a", "cv_b", "cv_c")[k - 1]], n + 1)
                if k == 3 and not isfirst(n):
                    dve.wait_ge(S["xc_rdy"], n)
                a, b = (cv0, cv1) if k % 2 else (cv1, cv0)
                inc(dve.scalar_tensor_tensor(b[:, :], src, v(V_CW + k), a[:, :], ALU.mult, ALU.add),
                    ("cv_b", "cv_c", "cv_rdy")[k - 1])

            def inputs(b, g):
                dve.wait_ge(S["u_bc"], stepno(b, g))
                if g == 0:
                    dve.wait_ge(S["b_row_rdy"], 16 * (b + 1))
                if not (isfirst(b) and g < 2):
                    dve.wait_ge(S["scan_done"], stepno(b, g) - 2)
                inc(dve.tensor_tensor(dbu[:, g % 2, :], u_ps[:, :], b_row[:, slot(b)], ALU.mult), "dbu_rdy")

            def scan(b, g):
                dve.wait_ge(S["da_rdy"], stepno(b, g))
                dve.wait_ge(S["dbu_rdy"], stepno(b, g))
                if not (isfirst(b) and g < RING):
                    dve.wait_ge(S["hc_rdy"], stepno(b, g) - RING)
                    dve.wait_ge(S["sums_done"], b * NQ + g // NQ - 1)
                inc(dve.tensor_tensor_scan(hs[:, g % RING, :], da_ps[g % 2][:, :], dbu[:, g % 2, :], 0.0,
                                           ALU.mult, ALU.add), "scan_done")

            def gated(b, e):
                dve.wait_ge(S["g_bc"], stepno(b, e))
                if not (isfirst(b) and e < 2):
                    dve.wait_ge(S["ffn_done"], stepno(b, e) - 2)
                inc(dve.tensor_tensor(xg[:, e % 2, :], g_ps[:, :], xn_ch[:, cols(b)], ALU.mult), "xg_rdy")

            def y_sum(b):
                dve.wait_ge(S["sums_done"], NQ * b + NQ)
                dve.wait_ge(S["xc_rdy"], b + 1)
                if not isfirst(b):
                    dve.wait_ge(S["yn_rdy"], b)
                inc(dve.scalar_tensor_tensor(yv[:, :], xc[:, slot(b)], v(V_D), y_ps[:, :], ALU.mult, ALU.add), "yv_rdy")

            def s_sum(b):
                dve.wait_ge(S["sgs_rdy"], b + 1)
                if not isfirst(b):
                    dve.wait_ge(S["pe_out"], b)
                inc(dve.tensor_tensor(sv[:, :], s_ps[:, :], sgs[:, slot(b)], ALU.mult), "sv_rdy")

            def gn1(b):
                dve.wait_ge(S["yv_rdy"], b + 1)
                inc(dve.bn_stats(gst[:, :], yv[:, :]), "gn_stats")

            def gn2(b):
                wait_apart(dve, ("gn_stats", b + 1))
                inc(dve.bn_aggr(gmv[:, :], gst[:, :]), "gn_mv")

            def gn3(b):
                dve.wait_ge(S["pe_gmu"], b + 1)
                inc(dve.tensor_copy(gm[:, :], y_ps[:, 0:2]), "gn_mu")

            def gn4(b):
                dve.wait_ge(S["gn_mu"], b + 1)
                inc(dve.tensor_tensor(dm[:, :], gmv[:, 0:1], gm[:, 0:1], ALU.subtract), "gn_dm")
                dve.wait_ge(S["gn_dm"], b + 1)
                inc(dve.tensor_tensor(dm2[:, :], dm[:, :], dm[:, :], ALU.mult), "gn_dm2")

            def gn5(b):
                dve.wait_ge(S["pe_gvar"], b + 1)
                inc(dve.tensor_tensor(gvar[:, :], y_ps[:, 0:1], gm[:, 1:2], ALU.add), "gn_var")

            def gn6(b):
                dve.wait_ge(S["gn_rstd"], b + 1)
                inc(dve.tensor_tensor(ga[:, :], gr[:, :], v(V_GG), ALU.mult), "gn_a")
                dve.wait_ge(S["gn_a"], b + 1)
                inc(dve.tensor_tensor(gma[:, :], gm[:, 0:1], ga[:, :], ALU.mult), "gn_ma")
                dve.wait_ge(S["gn_ma"], b + 1)
                inc(dve.tensor_tensor(gc[:, :], v(V_GB), gma[:, :], ALU.subtract), "gn_c")

            def plus_u(b):
                dve.wait_ge(S["pe_out"], b + 1)
                if not isfirst(b):
                    dve.wait_ge(S["o2_rdy"], b)
                inc(dve.tensor_tensor(o1[:, :], work[:, :], xn_ch[:, cols(b)], ALU.add), "o1_rdy")

            def sequence(b, before, after):
                n = b + 1
                for g in range(NG):
                    if g < NG - 1 or after:
                        inputs(*ahead(b, g, 1))
                    if before:
                        if g == 3:
                            y_sum(b - 1)
                        if g == 4:
                            gn2(b - 1)
                        if g == 5:
                            gn3(b - 1)
                        if g == 6:
                            gn5(b - 1)
                        if g == 7:
                            gn6(b - 1)
                    if after:
                        if g == 5:
                            conv(n, 2)
                        if g == 6:
                            rt1(n)
                        if g == 8:
                            rt4(n)
                        if g == 9:
                            rt7(n)
                        if g == 10:
                            rt10(n)
                        if g == 11:
                            rt13(n)
                    scan(b, g)
                    if before:
                        if g == 3:
                            s_sum(b - 1)
                        if g == 5:
                            gn4(b - 1)
                    if after:
                        if g == 4:
                            conv(n, 1)
                        if g == 6:
                            rt2(n)
                        if g == 8:
                            rt5(n)
                        if g == 9:
                            rt8(n)
                        if g == 10:
                            rt11(n)
                        if g == 11:
                            rt14(n)
                    gated(b, g)
                    if before:
                        if g == 3:
                            gn1(b - 1)
                        if g == 10:
                            plus_u(b - 1)
                    if after:
                        if g == 5:
                            conv(n, 3)
                        if g == 6:
                            rt3(n)
                        if g == 8:
                            rt6(n)
                        if g == 9:
                            rt9(n)
                        if g == 10:
                            rt12(n)

            dve.wait_ge(S["x0_in"], 16)
            ln_stats(1, 0, 1)
            dve.wait_ge(S["cst_in"], 16)
            dve.tensor_copy(sel_ch[:, :, :, :], cst[:, C_B:C_B + NQ * NI].rearrange(
                "p (q i) -> p q i", q=NQ).unsqueeze(2).to_broadcast([128, NQ, DS, NI]))
            dve.tensor_copy(ident_b[:, :], ident).then_inc(S["consts_ready"], 1)
            shifts(1, 0, 1)
            dve.wait_ge(S["x_in"], 16 * (B - 1))
            ln_stats(2, 1, B)
            dve.wait_ge(S["br_in"], 16)
            inc(dve.tensor_copy(br_parts[:, 0, :], br[:, :]), "br_hi")
            dve.wait_ge(S["br_hi"], 1)
            inc(dve.tensor_tensor(br_res[:, :], br[:, :], br_parts[:, 0, :], ALU.subtract), "br_left")
            dve.wait_ge(S["br_left"], 1)
            inc(dve.tensor_copy(br_parts[:, 1, :], br_res[:, :]), "br_mid")
            dve.wait_ge(S["br_mid"], 1)
            inc(dve.tensor_tensor(br_parts[:, 2, :], br_res[:, :], br_parts[:, 1, :], ALU.subtract), "br_lo")
            dve.tensor_copy(sel_ex[:, :, :], cst[0:SP3 * E, C_G:C_G + E].unsqueeze(2).to_broadcast(
                [SP3 * E, E, 128])).then_inc(S["consts_ready"], 1)
            dve.wait_ge(S["ws_in"], 16)
            dve.tensor_tensor(wsum[:, :], ws[:, 0, :], ws[:, 1, :], ALU.add).then_inc(S["set_dve"], 1)
            dve.wait_ge(S["set_dve"], 3)
            dve.scalar_tensor_tensor(wsum[:, :], wsum[:, :], 0.5, ident, ALU.mult, ALU.add).then_inc(
                S["consts_ready"], 1)
            dve.tensor_scalar(bias_sh[:, :], bias_sh[:, :], 0.5, None, ALU.mult).then_inc(S["set_dve"], 1)
            for k in range(1, KW):
                conv(0, k)
            shifts(2, 1, B)
            for rt in (rt1, rt2, rt3, rt4, rt5, rt6, rt7, rt8, rt9, rt10, rt11, rt12, rt13, rt14):
                rt(0)

            inputs(0, 0)
            sequence(0, False, True)
            with dve.Fori(1, B - 1) as b:
                sequence(b, True, True)
            sequence(B - 1, True, False)
            b = B - 1
            for piece in (y_sum, s_sum, gn1, gn2, gn3, gn4, gn5, gn6, plus_u):
                piece(b)

        @block.scalar
        def _(act):
            def go(name, dst, src, func, **kw):
                act.activation(dst, src, func, **kw).then_inc(S[name], 1)

            def sigmoid(part, n, names, t, src):
                if part == 0:
                    go(names[0], t, src, ACT.Exp, scale=-1.0)
                elif part == 1:
                    act.wait_ge(S[names[0]], n + 1)
                    go(names[1], t, t, ACT.Ln, bias=one_t[:, :])
                else:
                    act.wait_ge(S[names[1]], n + 1)
                    go(names[2], src, t, ACT.Exp, scale=-1.0)

            def rstd(n, need, mid, done, var, t):
                act.wait_ge(S[need], n + 1)
                go(mid, t, var, ACT.Ln, bias=eps_t[:, :])
                act.wait_ge(S[mid], n + 1)
                go(done, t, t, ACT.Exp, scale=-0.5)

            def normed(dst, n, r, nm, done):
                for t in range(TT):
                    tok = bass.ds(n * TT + t, 1)
                    ins = act.activation(dst[:, t, :], x_tok[:, n * TT + t, :], ACT.Identity,
                                         scale=r[:, tok], bias=nm[:, tok])
                ins.then_inc(S[done], 1)

            def ln1(n):
                act.wait_ge(S["ln1_shift"], 1 if isfirst(n) else 2)
                if not isfirst(n):
                    act.wait_ge(S["pe_xn"], n)
                normed(xn_tok, n, r1, nm1, "xn_tok_rdy")

            def ln2(n):
                act.wait_ge(S["ln2_shift"], 1 if isfirst(n) else 2)
                if not isfirst(n):
                    act.wait_ge(S["pe_h"], n)
                normed(xh_tok, n, r2, nm2, "xh_tok_rdy")

            def xn_out(n):
                act.wait_ge(S["pe_xn"], n + 1)
                act.activation(xn_now[:, :], work[:, :], ACT.Copy)
                go("xn_ch_rdy", xn_ch[:, cols(n)], work[:, :], ACT.Copy)

            def h_out(n):
                act.wait_ge(S["pe_h"], n + 1)
                go("h_ch_rdy", h_ch[:, cols(n)], work[:, :], ACT.Identity, scale=v(V_LG), bias=v(V_LB))

            def sp_1(n):
                act.wait_ge(S["pe_dt"], n + 1)
                if not isfirst(n):
                    act.wait_ge(S["dtv_rdy"], n)
                go("sp_pos", spp[:, :], work[:, :], ACT.Relu)
                go("sp_abs", sp[:, :], work[:, :], ACT.Abs)

            def sp_2(n):
                act.wait_ge(S["sp_abs"], n + 1)
                go("sp_exp", sp[:, :], sp[:, :], ACT.Exp, scale=-1.0)

            def sp_3(n):
                act.wait_ge(S["sp_exp"], n + 1)
                go("sp_ln", sp[:, :], sp[:, :], ACT.Ln, bias=one_t[:, :])

            def x_out(n):
                act.wait_ge(S["pe_x"], n + 1)
                act.wait_ge(S["set_dve"], 1)
                go("xpad_rdy", xpad[:, bass.ds(n * XP + KW - 1, L)], work[:, :], ACT.Copy)

            def conv_0(n):
                act.wait_ge(S["xpad_rdy"], n + 1)
                if not isfirst(n):
                    act.wait_ge(S["cv_c"], n)
                go("cv_a", cv0[:, :], xpad[:, bass.ds(n * XP, L)], ACT.Identity, scale=v(V_CW), bias=v(V_CB))

            def f_out(b):
                act.wait_ge(S["ffn_done"], stepno(b, E - 1))
                act.wait_ge(S["set_dve"], 4)
                if not isfirst(b):
                    act.wait_ge(S["gf_rdy"], b)
                go("fv_rdy", fv[:, :], f_ps[:, :], ACT.Identity, bias=bias_sh[:, :])

            SX = ("sx_e", "sx_l", "sx_rdy")

            def sx(part, n):
                if part == 0:
                    act.wait_ge(S["cv_rdy"], n + 1)
                    if not isfirst(n):
                        act.wait_ge(S["xc_rdy"], n)
                sigmoid(part, n, SX, sxv, cv1[:, :] if part == 0 else sxv)

            def zl_out(n):
                act.wait_ge(S["pe_z"], n + 1)
                if not isfirst(n):
                    act.wait_ge(S["zs_rdy"], n)
                go("zl_rdy", zl[:, :], work[:, :], ACT.Copy)

            def szp(part, n):
                if part == 0:
                    act.wait_ge(S["zl_rdy"], n + 1)
                sigmoid(part, n, ("sz_e", "sz_l", "sz_rdy"), szv, zl[:, :] if part == 0 else szv)

            def sgp(part, n):
                if part == 0:
                    act.wait_ge(S["pe_sg"], n + 1)
                sigmoid(part, n, ("sg_e", "sg_l", "sgs_rdy"), sgv, work[:, :] if part == 0 else sgs[:, slot(n)])

            def sfp(part, b):
                if part == 0:
                    act.wait_ge(S["fv_rdy"], b + 1)
                    if not isfirst(b):
                        act.wait_ge(S["gf_rdy"], b)
                sigmoid(part, b, ("sf_e", "sf_l", "sf_rdy"), sfv, fv[:, :] if part == 0 else sfv)

            def bc_out(n):
                act.wait_ge(S["pe_sg"], n + 1)
                if not isfirst(n):
                    act.wait_ge(S["b_row_rdy"], 16 * n)
                    act.wait_ge(S["c_row_rdy"], 16 * n)
                go("bc_rows_rdy", bc_rows[:, :], work[0:64, :], ACT.Copy)

            def part_hi(n, need, done, src, dst, moved):
                act.wait_ge(S[need], n + 1)
                if not isfirst(n):
                    act.wait_ge(S[moved], 16 * SP3 * n)
                go(done, dst[:, 0, :], src[:, :], ACT.Copy)

            def part_mid(n, need, done, src, dst):
                act.wait_ge(S[need], n + 1)
                go(done, dst[:, 1, :], src[:, :], ACT.Copy)

            def rt_exp(n):
                act.wait_ge(S["rt_scm"], n + 1)
                go("rt_exp", se[:, :, :], scm[:, :, :], ACT.Exp)

            def g_parts_out(n):
                act.wait_ge(S["pe_gparts"], n + 1)
                go("g_parts_rdy", g_parts[:, slot(n)], work_b[0:SP3 * E, 0:L], ACT.Copy)

            def decay(b, g):
                act.wait_ge(S["dt_bc"], stepno(b, g))
                go("da_rdy", da_ps[g % 2][:, :], da_ps[g % 2][:, :], ACT.Exp, scale=a_neg[:, g:g + 1])

            def gn_apply(b):
                act.wait_ge(S["gn_c"], b + 1)
                act.wait_ge(S["yv_rdy"], b + 1)
                if not isfirst(b):
                    act.wait_ge(S["yg_rdy"], b)
                go("yn_rdy", yn[:, :], yv[:, :], ACT.Identity, scale=ga[:, :], bias=gc[:, :])

            def hi_dt(n):
                part_hi(n, "dtv_rdy", "dt_hi", dtv, dt3, "dt_parts_out")

            def hi_u(n):
                part_hi(n, "uv_rdy", "u_hi", uv, u3, "u_parts_out")

            def mid_dt(n):
                part_mid(n, "dt_res", "dt_mid", dtr, dt3)

            def mid_u(n):
                part_mid(n, "u_res", "u_mid", ur, u3)

            def ln_rstd(k, lo, hi):
                tok = slice(lo * TT, hi * TT)
                act.wait_ge(S["ln_mv"], k)
                go("ln1_log", r1[:, tok], mv1[:, tok, 1], ACT.Ln, bias=eps_t[:, :])
                go("ln2_log", r2[:, tok], mv1[:, tok, 1], ACT.Ln, scale=1.0 + EPS, bias=eps2_t[:, :])
                act.wait_ge(S["ln1_log"], k)
                go("ln1_rstd", r1[:, tok], r1[:, tok], ACT.Exp, scale=-0.5)
                act.wait_ge(S["ln2_log"], k)
                go("ln2_rstd", r2[:, tok], r2[:, tok], ACT.Exp, scale=-0.5)

            def sequence(b, before, after):
                n = b + 1
                for g in range(NG):
                    if g < NG - 1 or after:
                        decay(*ahead(b, g, 1))
                    if before:
                        if g == 0:
                            f_out(b - 1)
                        if g == 2:
                            sfp(0, b - 1)
                            sfp(1, b - 1)
                            sfp(2, b - 1)
                        if g == 6:
                            rstd(b - 1, "gn_var", "gn_log", "gn_rstd", gvar[:, :], gr[:, :])
                        if g == 7:
                            gn_apply(b - 1)
                    if g == 0:
                        zl_out(b)
                    if g == 5:
                        szp(0, b)
                        szp(1, b)
                        szp(2, b)
                    if after:
                        if g == 0:
                            ln1(n)
                        if g == 1:
                            ln2(n)
                            xn_out(n)
                        if g == 2:
                            h_out(n)
                        if g == 3:
                            x_out(n)
                            conv_0(n)
                        if g == 4:
                            sp_1(n)
                            sp_2(n)
                            sp_3(n)
                        if g == 6:
                            hi_dt(n)
                            sx(0, n)
                            sx(1, n)
                            sx(2, n)
                        if g == 7:
                            rt_exp(n)
                            bc_out(n)
                            sgp(0, n)
                            mid_dt(n)
                        if g == 8:
                            hi_u(n)
                        if g == 9:
                            mid_u(n)
                        if g == 10:
                            sgp(1, n)
                            sgp(2, n)
                        if g == 13:
                            g_parts_out(n)

            act.preload_act_table_set("natural_log_exp_and_others")
            act.wait_ge(S["vec_in"], 16)
            go("set_act", a_neg[:, :], v(V_A, NG), ACT.Exp)
            act.wait_ge(S["set_act"], 1)
            go("set_act", a_neg[:, :], a_neg[:, :], ACT.Copy, scale=-1.0)
            act.wait_ge(S["set_dve"], 1)
            ln_rstd(1, 0, 1)
            ln1(0)
            ln2(0)
            xn_out(0)
            h_out(0)
            x_out(0)
            conv_0(0)
            sp_1(0)
            bc_out(0)
            sgp(0, 0)
            sp_2(0)
            sp_3(0)
            ln_rstd(2, 1, B)
            sx(0, 0)
            sx(1, 0)
            sx(2, 0)
            hi_dt(0)
            rt_exp(0)
            mid_dt(0)
            hi_u(0)
            mid_u(0)
            g_parts_out(0)
            sgp(1, 0)
            sgp(2, 0)
            act.wait_ge(S["set_act"], 2)
            decay(0, 0)
            sequence(0, False, True)
            with act.Fori(1, B - 1) as b:
                sequence(b, True, True)
            sequence(B - 1, True, False)
            f_out(B - 1)
            for part in range(3):
                sfp(part, B - 1)
            rstd(B - 1, "gn_var", "gn_log", "gn_rstd", gvar[:, :], gr[:, :])
            gn_apply(B - 1)

        @block.gpsimd
        def _(pool):
            def tt(name, dst, a, b, op):
                pool.tensor_tensor(dst, a, b, op).then_inc(S[name], 1)

            def outputs(b, g):
                waits = [("scan_done", stepno(b, g))]
                if g == 0:
                    waits.append(("c_row_rdy", 16 * (b + 1)))
                if not (isfirst(b) and g < RING):
                    waits.append(("sums_done", b * NQ + g // NQ - 1))
                wait_apart(pool, *waits)
                tt("hc_rdy", hc[:, g % RING, :], hs[:, g % RING, :], c_row[:, slot(b)], ALU.mult)

            def softplus(n):
                wait_apart(pool, ("sp_pos", n + 1), ("sp_ln", n + 1),
                           *([] if isfirst(n) else [("u_lo", n)]))
                tt("dtv_rdy", dtv[:, :], spp[:, :], sp[:, :], ALU.add)

            def dt_split(n, k):
                pool.wait_ge(S[("dt_hi", "dt_mid")[k]], n + 1)
                if k == 0:
                    tt("dt_res", dtr[:, :], dtv[:, :], dt3[:, 0, :], ALU.subtract)
                else:
                    tt("dt_lo", dt3[:, 2, :], dtr[:, :], dt3[:, 1, :], ALU.subtract)

            def u_split(n, k):
                pool.wait_ge(S[("u_hi", "u_mid")[k]], n + 1)
                if k == 0:
                    tt("u_res", ur[:, :], uv[:, :], u3[:, 0, :], ALU.subtract)
                else:
                    tt("u_lo", u3[:, 2, :], ur[:, :], u3[:, 1, :], ALU.subtract)

            def x_silu(n):
                wait_apart(pool, ("sx_rdy", n + 1), ("cv_rdy", n + 1))
                tt("xc_rdy", xc[:, slot(n)], cv1[:, :], sxv, ALU.mult)

            def x_dt(n):
                wait_apart(pool, ("xc_rdy", n + 1), ("dtv_rdy", n + 1))
                tt("uv_rdy", uv[:, :], dtv[:, :], xc[:, slot(n)], ALU.mult)

            def z_silu(n):
                wait_apart(pool, ("sz_rdy", n + 1))
                tt("zs_rdy", zs[:, slot(n)], zl[:, :], szv, ALU.mult)

            def f_silu(b):
                pool.wait_ge(S["sf_rdy"], b + 1)
                if not isfirst(b):
                    pool.wait_ge(S["o2_rdy"], b)
                tt("gf_rdy", gf[:, :], fv[:, :], sfv, ALU.mult)

            def y_gate(b):
                wait_apart(pool, ("yn_rdy", b + 1), ("zs_rdy", b + 1),
                           *([] if isfirst(b) else [("pe_out", b)]))
                tt("yg_rdy", yg[:, :], yn[:, :], zs[:, slot(b)], ALU.mult)

            def times_g(b):
                pool.wait_ge(S["o1_rdy"], b + 1)
                pool.wait_ge(S["gf_rdy"], b + 1)
                tt("o2_rdy", o2[:, :], o1[:, :], gf[:, :], ALU.mult)

            def plus_x(b):
                wait_apart(pool, ("o2_rdy", b + 1), ("xch_in", 16),
                           *([] if isfirst(b) else [("out_done", 16 * b)]))
                tt("o3_rdy", o3[:, :], o2[:, :], x_ch[:, cols(b)], ALU.add)

            def sequence(b, before, after):
                n = b + 1
                for g in range(NG):
                    outputs(b, g)
                    if before:
                        if g == 3:
                            f_silu(b - 1)
                        if g == 7:
                            y_gate(b - 1)
                        if g == 11:
                            times_g(b - 1)
                        if g == 14:
                            plus_x(b - 1)
                    if g == 5:
                        z_silu(b)
                    if after:
                        if g == 4:
                            softplus(n)
                        if g == 6:
                            dt_split(n, 0)
                            x_silu(n)
                        if g == 7:
                            dt_split(n, 1)
                            x_dt(n)
                        if g == 8:
                            u_split(n, 0)
                        if g == 9:
                            u_split(n, 1)

            softplus(0)
            x_silu(0)
            x_dt(0)
            dt_split(0, 0)
            u_split(0, 0)
            dt_split(0, 1)
            u_split(0, 1)
            sequence(0, False, True)
            with pool.Fori(1, B - 1) as b:
                sequence(b, True, True)
            sequence(B - 1, True, False)
            f_silu(B - 1)
            y_gate(B - 1)
            times_g(B - 1)
            plus_x(B - 1)

        @block.tensor
        def _(pe):
            def flip(n, src, rdy, after, done):
                pe.wait_ge(S[rdy], n + 1)
                after()
                for t in range(TT):
                    mm = pe.transpose(work[:, t * 128:(t + 1) * 128], src[:, t, :], ident)
                mm.then_inc(S[done], 1)

            def project(n, w, after, done):
                after()
                pe.matmul(work[:, :], win[:, w:w + D], h_ch[:, cols(n)], start=True, stop=True).then_inc(S[done], 1)

            def last(name, count):
                def wait():
                    pe.wait_ge(S[name], count)
                return wait

            def nothing():
                pass

            def scores(n, after):
                after()
                for t in range(TT):
                    mm = pe.matmul(work[:, t * E:(t + 1) * E], xn_now[:, t * 128:(t + 1) * 128],
                                   win[:, W_CEN:W_CEN + E], start=True, stop=True)
                mm.then_inc(S["pe_score"], 1)

            def gate_parts(n, after):
                wait_apart(pe, ("rt_lo", n + 1))
                after()
                for t in range(TT):
                    mm = pe.transpose(work_b[0:SP3 * E, t * 128:(t + 1) * 128],
                                      gate3[:, t, :, :].rearrange("p s e -> p (s e)"), ident_b[:, :])
                mm.then_inc(S["pe_gparts"], 1)

            def spread(b, g, ps, parts, now):
                q, j = divmod(g, NQ)
                if isfirst(b) and g < NQ:
                    for s in range(SP3):
                        mm = pe.matmul(ps, sel_ch[32 * j:32 * j + 32, q, :, :].rearrange("p n i -> p (n i)"),
                                       now[32 * j:32 * j + 32, s, :], start=(s == 0), stop=(s == SP3 - 1))
                    return mm
                return pe.matmul(ps, sel_ch[0:SP3 * 32, q, :, :].rearrange("p n i -> p (n i)"),
                                 parts[:, j, slot(b)], start=True, stop=True)

            def spread_dt(b, g):
                if isfirst(b):
                    if g == 0:
                        pe.wait_ge(S["dt_mid"], 1)
                        pe.wait_ge(S["dt_lo"], 1)
                    if g == NQ:
                        pe.wait_ge(S["dt_parts_rdy"], 16)
                elif g == 0:
                    pe.wait_ge(S["dt_parts_rdy"], 16 * (b + 1))
                if not (isfirst(b) and g < 2):
                    pe.wait_ge(S["scan_done"], stepno(b, g) - 2)
                spread(b, g, da_ps[g % 2][:, :], dt_parts, dt3).then_inc(S["dt_bc"], 1)

            def spread_u(b, g):
                if isfirst(b):
                    if g == 0:
                        pe.wait_ge(S["u_mid"], 1)
                        pe.wait_ge(S["u_lo"], 1)
                    if g == NQ:
                        pe.wait_ge(S["u_parts_rdy"], 16)
                elif g == 0:
                    pe.wait_ge(S["u_parts_rdy"], 16 * (b + 1))
                if not (isfirst(b) and g < 1):
                    pe.wait_ge(S["dbu_rdy"], stepno(b, g) - 1)
                spread(b, g, u_ps[:, :], u_parts, u3).then_inc(S["u_bc"], 1)

            def spread_gate(b, e):
                wait_apart(pe, *([("g_parts_rdy", b + 1)] if e == 0 else []),
                           *([] if isfirst(b) and e < 1 else [("xg_rdy", stepno(b, e) - 1)]))
                pe.matmul(g_ps[:, :], sel_ex[:, e, :], g_parts[:, slot(b)], start=True, stop=True).then_inc(S["g_bc"], 1)

            def expert(b, e):
                pe.wait_ge(S["xg_rdy"], stepno(b, e))
                mm = pe.matmul(f_ps[:, :], wr[:, e, :], xg[:, e % 2, :], start=False, stop=(e == E - 1))
                mm.then_inc(S["ffn_done"], 1)

            def shared(b):
                if not isfirst(b):
                    pe.wait_ge(S["fv_rdy"], b)
                else:
                    pe.wait_ge(S["consts_ready"], 3)
                    pe.wait_ge(S["wr_in"], 16)
                    pe.wait_ge(S["br_lo"], 1)
                pe.wait_ge(S["g_parts_rdy"], b + 1)
                pe.matmul(f_ps[:, :], wsum[:, :], xn_ch[:, cols(b)], start=True, stop=False)
                for k in range(SP3):
                    pe.matmul(f_ps[:, :], br_parts[:, k, :], g_parts[:, slot(b)], start=False, stop=False)

            def sums(b, q):
                pe.wait_ge(S["hc_rdy"], b * NG + NQ * (q + 1))
                if q == 0 and not isfirst(b):
                    pe.wait_ge(S["sv_rdy"], b)
                    pe.wait_ge(S["gn_var"], b)
                for j in range(NQ):
                    tile = slice(32 * j, 32 * j + 32)
                    pe.matmul(s_ps[tile, :], sel_s, hs[:, (NQ * q + j) % RING, :], start=(q == 0), stop=(q == NQ - 1))
                for j in range(NQ):
                    tile = slice(32 * j, 32 * j + 32)
                    mm = pe.matmul(y_ps[tile, :], sel_y[:, q, :], hc[:, (NQ * q + j) % RING, :],
                                   start=(q == 0), stop=(q == NQ - 1))
                mm.then_inc(S["sums_done"], 1)

            def gn_mean(b):
                pe.wait_ge(S["gn_mv"], b + 1)
                pe.matmul(y_ps[:, 0:2], g_avg, gmv[:, :], start=True, stop=True).then_inc(S["pe_gmu"], 1)

            def gn_spread(b):
                pe.wait_ge(S["gn_mu"], b + 1)
                pe.wait_ge(S["gn_dm2"], b + 1)
                pe.matmul(y_ps[:, 0:1], g_avg, dm2[:, :], start=True, stop=True).then_inc(S["pe_gvar"], 1)

            def out_rest(b, after):
                after()
                if isfirst(b):
                    pe.wait_ge(S["wout_in"], 16)
                pe.matmul(work[:, :], wout[:, O_RES:O_RES + D], h_ch[:, cols(b)], start=True, stop=False)
                pe.wait_ge(S["sv_rdy"], b + 1)
                pe.matmul(work[:, :], wout[:, O_S:O_S + D], sv[:, :], start=False, stop=False)

            def out_y(b):
                pe.wait_ge(S["yg_rdy"], b + 1)
                pe.matmul(work[:, :], wout[:, O_Y:O_Y + D], yg[:, :], start=False, stop=True).then_inc(S["pe_out"], 1)

            def sequence(b, before, after):
                n = b + 1
                for g in range(NG):
                    if g < NG - 2 or after:
                        spread_u(*ahead(b, g, 2))
                    if before and g == 0:
                        expert(b - 1, E - 1)
                    if g == 1:
                        shared(b)
                    if g >= 1:
                        expert(b, g - 1)
                    if g in (7, 10, 14):
                        sums(b, (g - 6) // 4)
                    if before and g == 2:
                        sums(b - 1, NQ - 1)
                    if g == 0:
                        project(b, W_Z, last("g_parts_rdy", b + 1), "pe_z")
                    if after and g == 1:
                        flip(n, xn_tok, "xn_tok_rdy", last("zl_rdy", n), "pe_xn")
                    if after and g == 2:
                        flip(n, xh_tok, "xh_tok_rdy", last("xn_ch_rdy", n + 1), "pe_h")
                    if after and g == 3:
                        project(n, W_X, last("h_ch_rdy", n + 1), "pe_x")
                    if before and g == 4:
                        gn_mean(b - 1)
                    if after and g == 4:
                        project(n, W_DT, last("xpad_rdy", n + 1), "pe_dt")
                    if before and g == 5:
                        gn_spread(b - 1)
                    if after and g == 5:
                        scores(n, last("sp_abs", n + 1))
                    if after and g == 6:
                        project(n, W_SBC, last("rt_sc", n + 1), "pe_sg")
                    if before and g == 8:
                        out_rest(b - 1, last("sg_e", n + 1) if after else last("zl_rdy", b + 1))
                    if before and g == 9:
                        out_y(b - 1)
                    if after and g == 13:
                        gate_parts(n, last("o1_rdy", b) if before else last("sg_e", n + 1))
                    if g < NG - 2 or after:
                        spread_dt(*ahead(b, g, 2))
                    if g < NG - 1 or after:
                        spread_gate(*ahead(b, g, 1))

            pe.wait_ge(S["cst_in"], 16)
            flip(0, xn_tok, "xn_tok_rdy", nothing, "pe_xn")
            flip(0, xh_tok, "xh_tok_rdy", last("xn_ch_rdy", 1), "pe_h")
            pe.wait_ge(S["win_in"], 16)
            project(0, W_X, last("h_ch_rdy", 1), "pe_x")
            project(0, W_DT, last("xpad_rdy", 1), "pe_dt")
            project(0, W_SBC, last("sp_abs", 1), "pe_sg")
            scores(0, last("sg_e", 1))
            pe.wait_ge(S["consts_ready"], 2)
            gate_parts(0, last("rt_sc", 1))
            spread_dt(0, 0)
            spread_u(0, 0)
            spread_gate(0, 0)
            spread_dt(0, 1)
            spread_u(0, 1)
            sequence(0, False, True)
            with pe.Fori(1, B - 1) as b:
                sequence(b, True, True)
            sequence(B - 1, True, False)
            expert(B - 1, E - 1)
            sums(B - 1, NQ - 1)
            out_rest(B - 1, last("o1_rdy", B - 1))
            gn_mean(B - 1)
            gn_spread(B - 1)
            out_y(B - 1)


def kernel(**inputs):
    import concourse.bacc as bacc
    from concourse.bass_utils import run_bass_kernel_spmd

    a = {k: np.asarray(val) for k, val in inputs.items()}
    x = np.ascontiguousarray(a["L0_attn_u"])

    def f(v):
        return np.asarray(v, np.float32)

    p = np.arange(128)
    const = np.zeros((128, C_END), np.float32)
    const[:, C_ID:C_ID + 128] = np.eye(128)
    const[:, C_AVG:C_AVG + 128] = (p[:, None] // DS == p[None, :] // DS) / (D // GN)
    for q in range(NQ):
        const[p, C_Y + 32 * q + NI * q + p % NI] = 1.0
        for s in range(NQ):
            for i in range(NI):
                const[32 * s + NI * q + i, C_B + NI * q + i] = 1.0
    const[p, C_S + p // NI] = 1.0 / D
    for s in range(SP3):
        const[E * s + np.arange(E), C_G + np.arange(E)] = 1.0

    w = a["L0_attn_in_proj_w"].T
    parts = {name: w[:, lo:hi] for name, lo, hi in (
        ("x", 0, D), ("z", D, 2 * D), ("dt", 2 * D, 3 * D), ("res", 3 * D, 4 * D),
        ("b", 4 * D, 4 * D + DS), ("c", 4 * D + DS, 4 * D + 2 * DS), ("sg", 4 * D + 2 * DS, 4 * D + 3 * DS))}
    sg_tiles = np.zeros((D, NQ, 32), np.float32)
    sg_tiles[:, :, 0:DS] = parts["sg"][:, None, :]
    sg_tiles[:, 0, DS:] = parts["b"]
    sg_tiles[:, 1, DS:] = parts["c"]
    w_in = np.concatenate([parts["dt"], parts["x"], parts["z"], sg_tiles.reshape(D, D), a["L0_ffn_centroids"].T], 1)
    wo = a["L0_attn_out_proj_w"].T
    wos = np.zeros((NQ, 32, D), np.float32)
    wos[:, 0:DS, :] = wo[None, D:D + DS, :]
    w_out = np.concatenate([parts["res"], wo[0:D], wos.reshape(D, D)], 1)
    a_rows = a["L0_attn_A_log"].reshape(NQ, NQ, NI, DS).transpose(3, 2, 1, 0).reshape(128, NG)
    vec = np.concatenate([
        a["L0_attn_conv_w"][:, 0, :], *[a["L0_attn_" + k][:, None] for k in
                                        ("conv_b", "ln_g", "ln_b", "gn_g", "gn_b", "D")],
        a["L0_ffn_bs"].T, a_rows, np.broadcast_to(a["L0_ffn_expert_biases"], (128, E))], 1)
    arrays = {
        "x": x, "xT": x.reshape(B * L, D).T, "const": const, "vec": vec, "w_in": w_in, "w_out": w_out,
        "w_r": a["L0_ffn_Wr"].transpose(2, 0, 1), "w_s": a["L0_ffn_Ws"].transpose(2, 0, 1), "b_r": np.tile(a["L0_ffn_br"], (SP3, 1)),
    }
    arrays = {k: np.ascontiguousarray(val) for k, val in arrays.items()}

    nc = bacc.Bacc("TRN2", target_bir_lowering=False, num_devices=1)
    args = [nc.dram_tensor(f"in_{k}", val.shape, mybir.dt.from_np(val.dtype), kind="ExternalInput").ap()
            for k, val in arrays.items()]
    args.append(nc.dram_tensor("out_ch", (D, B * L), F32, kind="ExternalOutput").ap())
    args += [nc.dram_tensor(name, (NQ, SP3 * 32, B * L), BF16, kind="Internal").ap() for name in ("dt_moved", "u_moved")]
    mamba_moe(nc, *args)
    r = run_bass_kernel_spmd(nc, [{f"in_{k}": val for k, val in arrays.items()}], core_ids=[0])
    return np.ascontiguousarray(r.results[0]["out_ch"].T.reshape(B, L, D))
```

```python
from contextlib import ExitStack

import numpy as np

import concourse.bass as bass
from concourse import mybir

F32 = mybir.dt.float32
BF16 = mybir.dt.bfloat16
ALU = mybir.AluOpType
ACT = mybir.ActivationFunctionType
AX = mybir.AxisListType.X

B, L, D = 4, 512, 128
DS, KW, GN = 16, 4, 8
E = 16
TT = L // 128
NI = D // DS
NG = D // NI
NQ = 4
SP3 = 3
RING = 2 * NQ
HALVES = (slice(0, L // 2), slice(L // 2, L))
DRING = 4
EPS = 1e-5
XP = L + KW - 1

C_ID, C_AVG, C_Y, C_S, C_B, C_G, C_END = np.cumsum([0, 128, 128, NQ * 32, 32, NQ * NI, E]).tolist()
W_DT, W_X, W_Z, W_SBC, W_CEN, W_END = np.cumsum([0] + [D] * 4 + [E]).tolist()
O_RES, O_Y, O_S, O_END = np.cumsum([0] + [D] * 3).tolist()
(V_CW, V_CB, V_LG, V_LB, V_GG, V_GB, V_D, V_BS, V_A, V_EB, V_END) = np.cumsum(
    [0, KW, 1, 1, 1, 1, 1, 1, 2, NG, E]).tolist()


def mamba_moe(nc, x, xT, const, vec, w_in, w_out, w_r, w_s, b_r, out, dt_moved, u_moved):
    with ExitStack() as ctx:
        def sb(name, shape, dt=F32):
            return ctx.enter_context(nc.sbuf_tensor(name, shape, dt))

        def pb(name):
            return ctx.enter_context(nc.psum_tensor(name, [128, L], F32))

        def sem(name):
            return ctx.enter_context(nc.semaphore(name))

        cst = sb("cst", [128, C_END])
        vecs = sb("vecs", [128, V_END])
        win = sb("win", [128, W_END])
        wout = sb("wout", [128, O_END])
        wr = sb("wr", [128, E, D])
        ws = sb("ws", [128, 2, D])
        wsum = sb("wsum", [128, D])
        br = sb("br", [SP3 * E, D]); br_res = sb("br_res", [SP3 * E, D])
        br_parts = sb("br_parts", [SP3 * E, SP3, D], BF16)
        ident_b = sb("ident_b", [128, 128], BF16)
        sel_ch = sb("sel_ch", [128, NQ, DS, NI], BF16)
        sel_ex = sb("sel_ex", [SP3 * E, E, 128], BF16)
        a_neg = sb("a_neg", [128, NG])
        bias_sh = sb("bias_sh", [128, 1])
        eps_t = sb("eps_t", [128, 1])
        eps2_t = sb("eps2_t", [128, 1])
        one_t = sb("one_t", [128, 1])
        ident = cst[:, C_ID:C_ID + 128]
        g_avg = cst[:, C_AVG:C_AVG + 128]
        sel_y = cst[:, C_Y:C_Y + NQ * 32].rearrange("p (q m) -> p q m", q=NQ)
        sel_s = cst[:, C_S:C_S + 32]

        def v(i, n=1):
            return vecs[:, i:i + n]

        x_tok = sb("x_tok", [128, B * TT, D])
        x_ch = sb("x_ch", [128, B * L])
        xn_ch = sb("xn_ch", [128, B * L])
        h_ch = sb("h_ch", [128, B * L])
        bc_rows = sb("bc_rows", [64, L])
        xpad = sb("xpad", [128, B * XP])

        xc = sb("xc", [128, 2 * L])
        zs = sb("zs", [128, 2 * L])
        sgs = sb("sgs", [128, 2 * L])
        b_row = sb("b_row", [128, 2 * L])
        c_row = sb("c_row", [128, 2 * L])
        g_parts = sb("g_parts", [SP3 * E, 2 * L], BF16)
        dt_parts = sb("dt_parts", [SP3 * 32, NQ, 2 * L], BF16)
        u_parts = sb("u_parts", [SP3 * 32, NQ, 2 * L], BF16)

        st1 = sb("st1", [128, B * TT, 6]); mv1 = sb("mv1", [128, B * TT, 2])
        r1 = sb("r1", [128, B * TT]); r2 = sb("r2", [128, B * TT])
        nm1 = sb("nm1", [128, B * TT]); nm2 = sb("nm2", [128, B * TT])

        xn_tok = sb("xn_tok", [128, TT, D])
        xn_now = sb("xn_now", [128, L])
        xh_tok = sb("xh_tok", [128, TT, D])
        sc = sb("sc", [128, TT, E]); scm = sb("scm", [128, TT, E]); se = sb("se", [128, TT, E])
        mx = sb("mx", [128, TT]); sm = sb("sm", [128, TT]); rs = sb("rs", [128, TT])
        pr = sb("pr", [128, TT, E]); top8 = sb("top8", [128, TT, 8]); top2 = sb("top2", [128, TT, 8])
        rest = sb("rest", [128, TT, E]); gate = sb("gate", [128, TT, E]); gres = sb("gres", [128, TT, E])
        gate3 = sb("gate3", [128, TT, SP3, E], BF16)
        spp = sb("spp", [128, L]); sp = sb("sp", [128, L]); dtv = sb("dtv", [128, L]); uv = sb("uv", [128, L])
        dt3 = sb("dt3", [128, SP3, L], BF16); u3 = sb("u3", [128, SP3, L], BF16)
        dtr = sb("dtr", [128, L]); ur = sb("ur", [128, L])
        cv0 = sb("cv0", [128, L]); cv1 = sb("cv1", [128, L])
        sx_t = sb("sx_t", [128, L]); zl = sb("zl", [128, L]); sz_t = sb("sz_t", [128, L]); sg_t = sb("sg_t", [128, L])
        fv = sb("fv", [128, L]); sf_t = sb("sf_t", [128, L]); gf = sb("gf", [128, L])
        yv = sb("yv", [128, L]); sv = sb("sv", [128, L]); yn = sb("yn", [128, L]); yg = sb("yg", [128, L])
        gst = sb("gst", [128, 6]); gmv = sb("gmv", [128, 2]); gm = sb("gm", [128, 2])
        dm = sb("dm", [128, 1]); dm2 = sb("dm2", [128, 1]); gvar = sb("gvar", [128, 1]); gr = sb("gr", [128, 1])
        ga = sb("ga", [128, 1]); gma = sb("gma", [128, 1]); gc = sb("gc", [128, 1])
        o1 = sb("o1", [128, L]); o3 = sb("o3", [128, L])
        da = sb("da", [128, DRING, L])
        dbu = sb("dbu", [128, 2, L])
        hs = sb("hs", [128, RING, L])
        hc = sb("hc", [128, RING, L])
        xg = sb("xg", [128, 2, L])
        idle_b = hc[:, RING - 1, :].bitcast(BF16)[:, 0:L]

        da_ps = pb("da_ps")
        u_ps = [pb("u_ps0"), pb("u_ps1")]
        g_ps = pb("g_ps")
        f_ps = pb("f_ps")
        y_ps = pb("y_ps")
        s_ps = pb("s_ps")
        work = pb("work")
        LAST_BANKS = (work, g_ps)
        work_b = work[:, :].bitcast(BF16)

        def bank(n, first):
            return first if isinstance(n, int) and n == 0 else work

        names = """
        cst_in vec_in win_in wout_in wr_in ws_in br_in x0_in x_in xch_in
        set_dve set_act set_pool consts_ready
        ln_stats ln_mv ln1_log ln1_rstd ln1_shift xn_tok_rdy ln2_log ln2_rstd ln2_shift xh_tok_rdy
        pe_xn xn_ch_rdy pe_h h_ch_rdy
        pe_score rt_sc rt_mx rt_scm rt_exp rt_sum rt_rcp rt_pr rt_top rt_top2 rt_rest rt_gate rt_hi rt_res rt_mid rt_lo
        pe_gparts g_parts_rdy br_hi br_mid br_lo br_left
        pe_dt sp_pos sp_abs sp_exp sp_ln dtv_rdy pe_x xpad_rdy cv_a cv_b cv_c cv_rdy sx_e sx_l sx_rdy xc_rdy uv_rdy
        dt_hi dt_res dt_mid dt_lo u_hi u_res u_mid u_lo dt_parts_out u_parts_out dt_parts_rdy u_parts_rdy
        pe_z zl_rdy sz_e sz_l sz_rdy zs_rdy pe_sg sg_e sg_l sgs_rdy bc_rows_rdy b_row_rdy c_row_rdy
        dt_bc da_rdy u_bc dbu_rdy scan_done hc_rdy last_hc_rdy means_done sums_done
        g_bc xg_rdy ffn_done
        fv_rdy sf_e sf_l sf_rdy gf_rdy yv_rdy sv_rdy gn_stats gn_mv pe_gmu gn_mu gn_dm gn_dm2 pe_gvar gn_var
        gn_log gn_rstd gn_a gn_ma gn_c yn_rdy yg_rdy pe_out o1_rdy o2_rdy gfx_rdy rest_rdy o3_rdy out_done
        """.split()
        S = {n: sem(n) for n in names}

        def cols(b):
            return bass.ts(b, L)

        def slot(b):
            return bass.ts(b % 2, L)

        def stepno(b, g):
            return b * NG + (g + 1)

        def ahead(b, g, k):
            return (b, g + k) if g + k < NG else (b + 1, g + k - NG)

        def isfirst(b):
            return isinstance(b, int) and b == 0

        def wait_apart(eng, *pairs):
            pairs = [(name, val if isinstance(val, int) else eng.compute_val(val)) for name, val in pairs]
            eng.wait_ge(S["set_dve"], 1)
            for name, val in pairs:
                eng.wait_ge(S[name], val)

        block = ctx.enter_context(nc.Block())

        @block.sync
        def _(eng):
            eng.dma_start(x_tok[:, 0:TT, :], x[0].rearrange("(t p) d -> p t d", p=128)).then_inc(S["x0_in"], 16)
            eng.dma_start(vecs[:, :], vec).then_inc(S["vec_in"], 16)
            eng.dma_start(cst[:, :], const).then_inc(S["cst_in"], 16)
            eng.dma_start(win[:, :], w_in).then_inc(S["win_in"], 16)
            eng.dma_start(ws[:, :, :], w_s).then_inc(S["ws_in"], 16)
            for b in range(1, B):
                eng.dma_start(x_tok[:, b * TT:(b + 1) * TT, :],
                              x[b].rearrange("(t p) d -> p t d", p=128)).then_inc(S["x_in"], 16)
            eng.dma_start(wr[:, :, :], w_r).then_inc(S["wr_in"], 16)
            eng.dma_start(br[:, :], b_r).then_inc(S["br_in"], 16)
            eng.dma_start(wout[:, :], w_out).then_inc(S["wout_in"], 16)
            eng.dma_start(x_ch[:, :], xT).then_inc(S["xch_in"], 16)

            def parts_out(n, src, moved, out_rdy, parts):
                for s, part in enumerate(parts):
                    wait_apart(eng, (part, n + 1))
                    eng.dma_start(moved[:, 32 * s:32 * s + 32, cols(n)], src[:, s, :]).then_inc(S[out_rdy], 16)

            def parts_in(n, dst, moved, out_rdy, rdy):
                wait_apart(eng, (out_rdy, 16 * SP3 * (n + 1)))
                eng.dma_start(dst[:, :, slot(n)], moved[:, :, cols(n)].rearrange("j r t -> r j t")).then_inc(S[rdy], 16)

            def bc_spread(n):
                wait_apart(eng, ("bc_rows_rdy", n + 1))
                for dst, lo, rdy in ((b_row, 16, "b_row_rdy"), (c_row, 48, "c_row_rdy")):
                    eng.dma_start(dst[:, slot(n)], bc_rows[lo:lo + DS, :].unsqueeze(1).to_broadcast(
                        [DS, NI, L])).then_inc(S[rdy], 16)

            def moves(n):
                if isfirst(n):
                    bc_spread(n)
                parts_out(n, dt3, dt_moved, "dt_parts_out", ("dt_hi", "dt_mid", "dt_lo"))
                if not isfirst(n):
                    bc_spread(n)
                parts_out(n, u3, u_moved, "u_parts_out", ("u_hi", "u_mid", "u_lo"))
                parts_in(n, dt_parts, dt_moved, "dt_parts_out", "dt_parts_rdy")
                parts_in(n, u_parts, u_moved, "u_parts_out", "u_parts_rdy")

            def store(b):
                wait_apart(eng, ("o3_rdy", b + 1))
                eng.dma_start(out[:, cols(b)], o3[:, :]).then_inc(S["out_done"], 16)

            moves(0)
            moves(1)
            with eng.Fori(1, B - 1) as b:
                moves(b + 1)
                store(b - 1)
            store(B - 2)
            for k, half in enumerate(HALVES):
                eng.wait_ge(S["o3_rdy"], B + k)
                eng.dma_start(out[:, (B - 1) * L:][:, half], o3[:, half]).then_inc(S["out_done"], 16)
            eng.wait_ge(S["out_done"], 16 * (B + 1))

        @block.vector
        def _(dve):
            def inc(ins, name):
                ins.then_inc(S[name], 1)

            dve.memset(eps_t[:, :], EPS)
            dve.memset(eps2_t[:, :], EPS * EPS)
            dve.memset(one_t[:, :], 1.0)
            dve.memset(top2[:, :, :], -1.0)
            inc(dve.memset(xpad[:, :].rearrange("p (b t) -> p b t", b=B)[:, :, 0:KW - 1], 0.0), "set_dve")

            def ln_stats(n):
                for t in range(n * TT, (n + 1) * TT):
                    last = dve.bn_stats(st1[:, t, :], x_tok[:, t, :])
                inc(last, "ln_stats")
                wait_apart(dve, ("ln_stats", n + 1))
                for t in range(n * TT, (n + 1) * TT):
                    last = dve.bn_aggr(mv1[:, t, :], st1[:, t, :])
                inc(last, "ln_mv")

            def shifts(n):
                tok = slice(n * TT, (n + 1) * TT)
                dve.wait_ge(S["ln_mv"], n + 1)
                for r, nm, rdy, done in ((r1, nm1, "ln1_rstd", "ln1_shift"), (r2, nm2, "ln2_rstd", "ln2_shift")):
                    dve.wait_ge(S[rdy], n + 1)
                    inc(dve.scalar_tensor_tensor(nm[:, tok], mv1[:, tok, 0], -1.0, r[:, tok], ALU.mult, ALU.mult), done)

            def bc_e(t2):
                return t2[:, :].unsqueeze(2).to_broadcast([128, TT, E])

            def biased_scores(n):
                dve.wait_ge(S["pe_score"], n + 1)
                inc(dve.tensor_tensor(sc[:, :, :], bank(n, s_ps)[:, 0:TT * E].rearrange("p (t e) -> p t e", e=E),
                                      v(V_EB, E).unsqueeze(1).to_broadcast([128, TT, E]), ALU.add), "rt_sc")

            def score_max(n):
                dve.wait_ge(S["rt_sc"], n + 1)
                inc(dve.tensor_reduce(mx[:, :], sc[:, :, :], AX, ALU.max), "rt_mx")

            def less_max(n):
                dve.wait_ge(S["rt_mx"], n + 1)
                inc(dve.tensor_tensor(scm[:, :, :], sc[:, :, :], bc_e(mx), ALU.subtract), "rt_scm")

            def exp_sum(n):
                dve.wait_ge(S["rt_exp"], n + 1)
                inc(dve.tensor_reduce(sm[:, :], se[:, :, :], AX, ALU.add), "rt_sum")

            def sum_inverse(n):
                dve.wait_ge(S["rt_sum"], n + 1)
                inc(dve.reciprocal(rs[:, :], sm[:, :]), "rt_rcp")

            def probabilities(n):
                dve.wait_ge(S["rt_rcp"], n + 1)
                inc(dve.tensor_tensor(pr[:, :, :], se[:, :, :], bc_e(rs), ALU.mult), "rt_pr")

            def top_eight(n):
                wait_apart(dve, ("rt_pr", n + 1))
                for t in range(TT):
                    last = dve.max(top8[:, t, :], pr[:, t, :])
                inc(last, "rt_top")

            def top_two(n):
                dve.wait_ge(S["rt_top"], n + 1)
                inc(dve.tensor_copy(top2[:, :, 0:2], top8[:, :, 0:2]), "rt_top2")

            def without_top_two(n):
                wait_apart(dve, ("rt_top2", n + 1))
                for t in range(TT):
                    last = dve.match_replace(rest[:, t, :], top2[:, t, :], pr[:, t, :], 0.0)
                inc(last, "rt_rest")

            def best_gates(n):
                dve.wait_ge(S["rt_rest"], n + 1)
                inc(dve.tensor_tensor(gate[:, :, :], pr[:, :, :], rest[:, :, :], ALU.subtract), "rt_gate")

            def gates_hi(n):
                dve.wait_ge(S["rt_gate"], n + 1)
                if not isfirst(n):
                    dve.wait_ge(S["pe_gparts"], n)
                inc(dve.tensor_copy(gate3[:, :, 0, :], gate[:, :, :]), "rt_hi")

            def gates_left(n):
                dve.wait_ge(S["rt_hi"], n + 1)
                inc(dve.tensor_tensor(gres[:, :, :], gate[:, :, :], gate3[:, :, 0, :], ALU.subtract), "rt_res")

            def gates_mid(n):
                dve.wait_ge(S["rt_res"], n + 1)
                inc(dve.tensor_copy(gate3[:, :, 1, :], gres[:, :, :]), "rt_mid")

            def gates_lo(n):
                dve.wait_ge(S["rt_mid"], n + 1)
                inc(dve.tensor_tensor(gate3[:, :, 2, :], gres[:, :, :], gate3[:, :, 1, :], ALU.subtract), "rt_lo")

            def conv(n, k):
                src = xpad[:, bass.ds(n * XP + k, L)]
                dve.wait_ge(S[("cv_a", "cv_b", "cv_c")[k - 1]], n + 1)
                if k == 3 and not isfirst(n):
                    dve.wait_ge(S["xc_rdy"], n)
                a, b = (cv0, cv1) if k % 2 else (cv1, cv0)
                inc(dve.scalar_tensor_tensor(b[:, :], src, v(V_CW + k), a[:, :], ALU.mult, ALU.add),
                    ("cv_b", "cv_c", "cv_rdy")[k - 1])

            def dt_lo(n):
                dve.wait_ge(S["dt_mid"], n + 1)
                inc(dve.tensor_tensor(dt3[:, 2, :], dtr[:, :], dt3[:, 1, :], ALU.subtract), "dt_lo")

            def inputs(b, g):
                dve.wait_ge(S["u_bc"], stepno(b, g))
                if g == 0:
                    dve.wait_ge(S["b_row_rdy"], 16 * (b + 1))
                if not (isfirst(b) and g < 2):
                    dve.wait_ge(S["scan_done"], stepno(b, g) - 2)
                inc(dve.tensor_tensor(dbu[:, g % 2, :], u_ps[g % 2][:, :], b_row[:, slot(b)], ALU.mult), "dbu_rdy")

            def scan(b, g):
                dve.wait_ge(S["da_rdy"], stepno(b, g))
                dve.wait_ge(S["dbu_rdy"], stepno(b, g))
                if not (isfirst(b) and g < RING):
                    dve.wait_ge(S["hc_rdy"], stepno(b, g) - RING)
                    dve.wait_ge(S["sums_done"], b * NQ + g // NQ - 1)
                inc(dve.tensor_tensor_scan(hs[:, g % RING, :], da[:, g % DRING, :], dbu[:, g % 2, :], 0.0,
                                           ALU.mult, ALU.add), "scan_done")

            def last_output():
                b, g = B - 1, NG - 1
                dve.wait_ge(S["scan_done"], stepno(b, g))
                inc(dve.tensor_tensor(hc[:, g % RING, :], hs[:, g % RING, :], c_row[:, slot(b)], ALU.mult),
                    "last_hc_rdy")

            def gated(b, e):
                dve.wait_ge(S["g_bc"], stepno(b, e))
                if not (isfirst(b) and e < 2):
                    dve.wait_ge(S["ffn_done"], stepno(b, e) - 2)
                inc(dve.tensor_tensor(xg[:, e % 2, :], g_ps[:, :], xn_ch[:, cols(b)], ALU.mult), "xg_rdy")

            def y_sum(b):
                dve.wait_ge(S["sums_done"], NQ * b + NQ)
                dve.wait_ge(S["xc_rdy"], b + 1)
                if not isfirst(b):
                    dve.wait_ge(S["yn_rdy"], b)
                inc(dve.scalar_tensor_tensor(yv[:, :], xc[:, slot(b)], v(V_D), y_ps[:, :], ALU.mult, ALU.add), "yv_rdy")

            def s_sum(b):
                dve.wait_ge(S["means_done"], NQ * b + NQ)
                dve.wait_ge(S["sgs_rdy"], b + 1)
                if not isfirst(b):
                    dve.wait_ge(S["pe_out"], b)
                inc(dve.tensor_tensor(sv[:, :], s_ps[:, :], sgs[:, slot(b)], ALU.mult), "sv_rdy")

            def channel_stats(b):
                dve.wait_ge(S["yv_rdy"], b + 1)
                inc(dve.bn_stats(gst[:, :], yv[:, :]), "gn_stats")

            def channel_mean_var(b):
                wait_apart(dve, ("gn_stats", b + 1))
                inc(dve.bn_aggr(gmv[:, :], gst[:, :]), "gn_mv")

            def group_mean(b):
                dve.wait_ge(S["pe_gmu"], b + 1)
                inc(dve.tensor_copy(gm[:, :], y_ps[:, 0:2]), "gn_mu")

            def mean_apart(b):
                dve.wait_ge(S["gn_mu"], b + 1)
                inc(dve.tensor_tensor(dm[:, :], gmv[:, 0:1], gm[:, 0:1], ALU.subtract), "gn_dm")
                dve.wait_ge(S["gn_dm"], b + 1)
                inc(dve.tensor_tensor(dm2[:, :], dm[:, :], dm[:, :], ALU.mult), "gn_dm2")

            def group_var(b):
                dve.wait_ge(S["pe_gvar"], b + 1)
                inc(dve.tensor_tensor(gvar[:, :], y_ps[:, 0:1], gm[:, 1:2], ALU.add), "gn_var")

            def norm_factors(b):
                dve.wait_ge(S["gn_rstd"], b + 1)
                inc(dve.tensor_tensor(ga[:, :], gr[:, :], v(V_GG), ALU.mult), "gn_a")
                dve.wait_ge(S["gn_a"], b + 1)
                inc(dve.tensor_tensor(gma[:, :], gm[:, 0:1], ga[:, :], ALU.mult), "gn_ma")
                dve.wait_ge(S["gn_ma"], b + 1)
                inc(dve.tensor_tensor(gc[:, :], v(V_GB), gma[:, :], ALU.subtract), "gn_c")

            def y_gate(b):
                dve.wait_ge(S["yn_rdy"], b + 1)
                dve.wait_ge(S["zs_rdy"], b + 1)
                inc(dve.tensor_tensor(yg[:, :], yn[:, :], zs[:, slot(b)], ALU.mult), "yg_rdy")

            def plus_u(b):
                dve.wait_ge(S["pe_out"], b + 1)
                if not isfirst(b):
                    dve.wait_ge(S["o3_rdy"], b)
                inc(dve.tensor_tensor(o1[:, :], work[:, :], xn_ch[:, cols(b)], ALU.add), "o1_rdy")

            def sequence(b, before, after):
                n = b + 1
                for g in range(NG):
                    if g < NG - 1 or after:
                        inputs(*ahead(b, g, 1))
                    if before:
                        if g == 2:
                            s_sum(b - 1)
                        if g == 3:
                            channel_stats(b - 1)
                        if g == 4:
                            channel_mean_var(b - 1)
                        if g == 5:
                            group_mean(b - 1)
                        if g == 6:
                            group_var(b - 1)
                        if g == 7:
                            norm_factors(b - 1)
                        if g == 9:
                            y_gate(b - 1)
                    if after:
                        if g == 5:
                            conv(n, 1)
                        if g == 6:
                            conv(n, 3)
                            biased_scores(n)
                        if g == 9:
                            dt_lo(n)
                            exp_sum(n)
                        if g == 10:
                            top_eight(n)
                        if g == 11:
                            best_gates(n)
                        if g == 12:
                            gates_mid(n)
                    scan(b, g)
                    if before:
                        if g == 5:
                            mean_apart(b - 1)
                    if after:
                        if g == 6:
                            score_max(n)
                        if g == 9:
                            sum_inverse(n)
                        if g == 10:
                            top_two(n)
                        if g == 11:
                            gates_hi(n)
                        if g == 12:
                            gates_lo(n)
                    if not after and g == NG - 1:
                        last_output()
                    gated(b, g)
                    if isfirst(b):
                        if g in (7, 10):
                            ln_stats({7: 2, 10: 3}[g])
                        if g in (9, 12):
                            shifts({9: 2, 12: 3}[g])
                    if before:
                        if g == 2:
                            y_sum(b - 1)
                        if g == 11:
                            plus_u(b - 1)
                    if after:
                        if g == 5:
                            conv(n, 2)
                        if g == 6:
                            less_max(n)
                        if g == 9:
                            probabilities(n)
                        if g == 10:
                            without_top_two(n)
                        if g == 11:
                            gates_left(n)

            dve.wait_ge(S["x0_in"], 16)
            ln_stats(0)
            dve.wait_ge(S["vec_in"], 16)
            dve.tensor_tensor(bias_sh[:, :], v(V_BS), v(V_BS + 1), ALU.add).then_inc(S["set_dve"], 1)
            dve.wait_ge(S["cst_in"], 16)
            dve.tensor_copy(sel_ch[:, :, :, :], cst[:, C_B:C_B + NQ * NI].rearrange(
                "p (q i) -> p q i", q=NQ).unsqueeze(2).to_broadcast([128, NQ, DS, NI]))
            dve.tensor_copy(ident_b[:, :], ident).then_inc(S["consts_ready"], 1)
            shifts(0)
            for t in range(TT):
                last = dve.tensor_scalar(xh_tok[:, t, :], x_tok[:, t, :], mv1[:, t, 0:1], r2[:, t:t + 1],
                                         ALU.subtract, ALU.mult)
            inc(last, "xh_tok_rdy")
            dve.tensor_copy(sel_ex[:, :, :], cst[0:SP3 * E, C_G:C_G + E].unsqueeze(2).to_broadcast(
                [SP3 * E, E, 128])).then_inc(S["consts_ready"], 1)
            dve.wait_ge(S["ws_in"], 16)
            dve.tensor_tensor(wsum[:, :], ws[:, 0, :], ws[:, 1, :], ALU.add).then_inc(S["set_dve"], 1)
            dve.wait_ge(S["set_dve"], 3)
            dve.scalar_tensor_tensor(wsum[:, :], wsum[:, :], 0.5, ident, ALU.mult, ALU.add).then_inc(
                S["consts_ready"], 1)
            dve.tensor_scalar(bias_sh[:, :], bias_sh[:, :], 0.5, None, ALU.mult).then_inc(S["set_dve"], 1)
            dve.wait_ge(S["x_in"], 16 * (B - 1))
            ln_stats(1)
            conv(0, 1)
            conv(0, 2)
            conv(0, 3)
            dve.wait_ge(S["br_in"], 16)
            inc(dve.tensor_copy(br_parts[:, 0, :], br[:, :]), "br_hi")
            dve.wait_ge(S["br_hi"], 1)
            inc(dve.tensor_tensor(br_res[:, :], br[:, :], br_parts[:, 0, :], ALU.subtract), "br_left")
            dve.wait_ge(S["br_left"], 1)
            inc(dve.tensor_copy(br_parts[:, 1, :], br_res[:, :]), "br_mid")
            dve.wait_ge(S["br_mid"], 1)
            inc(dve.tensor_tensor(br_parts[:, 2, :], br_res[:, :], br_parts[:, 1, :], ALU.subtract), "br_lo")

            biased_scores(0)
            dve.wait_ge(S["sp_pos"], 1)
            dve.wait_ge(S["sp_ln"], 1)
            inc(dve.tensor_tensor(dtv[:, :], spp[:, :], sp[:, :], ALU.add), "dtv_rdy")
            score_max(0)
            dve.wait_ge(S["dtv_rdy"], 1)
            inc(dve.tensor_copy(dt3[:, 0, :], dtv[:, :]), "dt_hi")
            less_max(0)
            dve.wait_ge(S["sx_rdy"], 1)
            inc(dve.tensor_tensor(xc[:, 0:L], cv1[:, :], sx_t[:, :], ALU.mult), "xc_rdy")
            exp_sum(0)
            dve.wait_ge(S["xc_rdy"], 1)
            inc(dve.tensor_tensor(uv[:, :], dtv[:, :], xc[:, 0:L], ALU.mult), "uv_rdy")
            sum_inverse(0)
            dve.wait_ge(S["uv_rdy"], 1)
            inc(dve.tensor_copy(u3[:, 0, :], uv[:, :]), "u_hi")
            probabilities(0)
            dve.wait_ge(S["u_hi"], 1)
            inc(dve.tensor_tensor(ur[:, :], uv[:, :], u3[:, 0, :], ALU.subtract), "u_res")
            dt_lo(0)
            dve.wait_ge(S["u_res"], 1)
            inc(dve.tensor_copy(u3[:, 1, :], ur[:, :]), "u_mid")
            top_eight(0)
            dve.wait_ge(S["u_mid"], 1)
            inc(dve.tensor_tensor(u3[:, 2, :], ur[:, :], u3[:, 1, :], ALU.subtract), "u_lo")
            for piece in (top_two, without_top_two, best_gates, gates_hi, gates_left, gates_mid, gates_lo):
                piece(0)
            shifts(1)

            inputs(0, 0)
            sequence(0, False, True)
            with dve.Fori(1, B - 1) as b:
                sequence(b, True, True)
            sequence(B - 1, True, False)
            b = B - 1
            for piece in (y_sum, channel_stats, channel_mean_var, group_mean, mean_apart, s_sum,
                          group_var, norm_factors):
                piece(b)
            dve.wait_ge(S["gn_c"], b + 1)
            for half in HALVES:
                inc(dve.tensor_scalar(yn[:, half], yv[:, half], ga[:, :], gc[:, :], ALU.mult, ALU.add), "yn_rdy")
            dve.wait_ge(S["zs_rdy"], b + 1)
            for k, half in enumerate(HALVES):
                dve.wait_ge(S["yn_rdy"], b + 1 + k)
                inc(dve.tensor_tensor(yg[:, half], yn[:, half], zs[:, (b % 2) * L:][:, half], ALU.mult), "yg_rdy")
            dve.wait_ge(S["gf_rdy"], b + 1)
            dve.wait_ge(S["out_done"], 16 * b)
            for k, (ps, half) in enumerate(zip(LAST_BANKS, HALVES)):
                dve.wait_ge(S["pe_out"], b + 1 + k)
                inc(dve.tensor_tensor(o3[:, half], ps[:, half], gf[:, half], ALU.mult), "o2_rdy")
                dve.wait_ge(S["o2_rdy"], b + 1 + k)
                dve.wait_ge(S["rest_rdy"], 1 + k)
                inc(dve.tensor_tensor(o3[:, half], o3[:, half], o1[:, half], ALU.add), "o3_rdy")

        @block.scalar
        def _(act):
            def go(name, dst, src, func, **kw):
                act.activation(dst, src, func, **kw).then_inc(S[name], 1)

            def sigmoid(part, n, names, t, src):
                if part == 0:
                    go(names[0], t, src, ACT.Exp, scale=-1.0)
                elif part == 1:
                    act.wait_ge(S[names[0]], n + 1)
                    go(names[1], t, t, ACT.Ln, bias=one_t[:, :])
                else:
                    act.wait_ge(S[names[1]], n + 1)
                    go(names[2], src, t, ACT.Exp, scale=-1.0)

            def rstd(n, need, mid, done, var, t):
                act.wait_ge(S[need], n + 1)
                go(mid, t, var, ACT.Ln, bias=eps_t[:, :])
                act.wait_ge(S[mid], n + 1)
                go(done, t, t, ACT.Exp, scale=-0.5)

            def normed(dst, n, r, nm, done):
                for t in range(TT):
                    tok = bass.ds(n * TT + t, 1)
                    ins = act.activation(dst[:, t, :], x_tok[:, n * TT + t, :], ACT.Identity,
                                         scale=r[:, tok], bias=nm[:, tok])
                ins.then_inc(S[done], 1)

            def ln1(n):
                act.wait_ge(S["ln1_shift"], n + 1)
                if not isfirst(n):
                    act.wait_ge(S["pe_xn"], n)
                normed(xn_tok, n, r1, nm1, "xn_tok_rdy")

            def ln2(n):
                act.wait_ge(S["ln2_shift"], n + 1)
                if not isfirst(n):
                    act.wait_ge(S["pe_h"], n)
                normed(xh_tok, n, r2, nm2, "xh_tok_rdy")

            def xn_out(n):
                act.wait_ge(S["pe_xn"], n + 1)
                act.activation(xn_now[:, :], work[:, :], ACT.Copy)
                go("xn_ch_rdy", xn_ch[:, cols(n)], work[:, :], ACT.Copy)

            def h_out(n):
                act.wait_ge(S["pe_h"], n + 1)
                go("h_ch_rdy", h_ch[:, cols(n)], bank(n, g_ps)[:, :], ACT.Identity, scale=v(V_LG), bias=v(V_LB))

            def softplus_sides(n):
                act.wait_ge(S["pe_dt"], n + 1)
                if not isfirst(n):
                    act.wait_ge(S["dtv_rdy"], n)
                go("sp_pos", spp[:, :], bank(n, da_ps)[:, :], ACT.Relu)
                go("sp_abs", sp[:, :], bank(n, da_ps)[:, :], ACT.Abs)

            def softplus_exp(n):
                act.wait_ge(S["sp_abs"], n + 1)
                go("sp_exp", sp[:, :], sp[:, :], ACT.Exp, scale=-1.0)

            def softplus_log(n):
                act.wait_ge(S["sp_exp"], n + 1)
                go("sp_ln", sp[:, :], sp[:, :], ACT.Ln, bias=one_t[:, :])

            def x_out(n):
                act.wait_ge(S["pe_x"], n + 1)
                act.wait_ge(S["set_dve"], 1)
                go("xpad_rdy", xpad[:, bass.ds(n * XP + KW - 1, L)], bank(n, u_ps[0])[:, :], ACT.Copy)

            def conv_0(n):
                act.wait_ge(S["xpad_rdy"], n + 1)
                if not isfirst(n):
                    act.wait_ge(S["cv_c"], n)
                go("cv_a", cv0[:, :], xpad[:, bass.ds(n * XP, L)], ACT.Identity, scale=v(V_CW), bias=v(V_CB))

            def f_out(b):
                act.wait_ge(S["ffn_done"], stepno(b, E - 1))
                act.wait_ge(S["set_dve"], 4)
                if not isfirst(b):
                    act.wait_ge(S["gf_rdy"], b)
                go("fv_rdy", fv[:, :], f_ps[:, :], ACT.Identity, bias=bias_sh[:, :])

            def conv_sigmoid(part, n):
                if part == 0:
                    act.wait_ge(S["cv_rdy"], n + 1)
                    if not isfirst(n):
                        act.wait_ge(S["xc_rdy"], n)
                sigmoid(part, n, ("sx_e", "sx_l", "sx_rdy"), sx_t[:, :], cv1[:, :] if part == 0 else sx_t[:, :])

            def zl_out(n):
                act.wait_ge(S["pe_z"], n + 1)
                if not isfirst(n):
                    act.wait_ge(S["zs_rdy"], n)
                go("zl_rdy", zl[:, :], work[:, :], ACT.Copy)

            def z_sigmoid(part, n):
                if part == 0:
                    act.wait_ge(S["zl_rdy"], n + 1)
                sigmoid(part, n, ("sz_e", "sz_l", "sz_rdy"), sz_t[:, :], zl[:, :] if part == 0 else sz_t[:, :])

            def state_sigmoid(part, n):
                if part == 0:
                    act.wait_ge(S["pe_sg"], n + 1)
                sigmoid(part, n, ("sg_e", "sg_l", "sgs_rdy"), sg_t[:, :],
                        bank(n, y_ps)[:, :] if part == 0 else sgs[:, slot(n)])

            def experts_sigmoid(part, b):
                if part == 0:
                    act.wait_ge(S["fv_rdy"], b + 1)
                    if not isfirst(b):
                        act.wait_ge(S["gf_rdy"], b)
                sigmoid(part, b, ("sf_e", "sf_l", "sf_rdy"), sf_t[:, :], fv[:, :] if part == 0 else sf_t[:, :])

            def bc_out(n):
                act.wait_ge(S["pe_sg"], n + 1)
                if not isfirst(n):
                    act.wait_ge(S["b_row_rdy"], 16 * n)
                    act.wait_ge(S["c_row_rdy"], 16 * n)
                go("bc_rows_rdy", bc_rows[:, :], bank(n, y_ps)[0:64, :], ACT.Copy)

            def part_hi(n, need, done, src, dst, moved):
                act.wait_ge(S[need], n + 1)
                if not isfirst(n):
                    act.wait_ge(S[moved], 16 * SP3 * n)
                go(done, dst[:, 0, :], src[:, :], ACT.Copy)

            def part_mid(n, need, done, src, dst):
                act.wait_ge(S[need], n + 1)
                go(done, dst[:, 1, :], src[:, :], ACT.Copy)

            def rt_exp(n):
                act.wait_ge(S["rt_scm"], n + 1)
                go("rt_exp", se[:, :, :], scm[:, :, :], ACT.Exp)

            def g_parts_out(n):
                act.wait_ge(S["pe_gparts"], n + 1)
                go("g_parts_rdy", g_parts[:, slot(n)], work_b[0:SP3 * E, 0:L], ACT.Copy)

            def decay(b, g):
                act.wait_ge(S["dt_bc"], stepno(b, g))
                if not (isfirst(b) and g < DRING):
                    act.wait_ge(S["scan_done"], stepno(b, g) - DRING)
                go("da_rdy", da[:, g % DRING, :], da_ps[:, :], ACT.Exp, scale=a_neg[:, g:g + 1])

            def gn_apply(b):
                act.wait_ge(S["gn_c"], b + 1)
                act.wait_ge(S["yv_rdy"], b + 1)
                if not isfirst(b):
                    act.wait_ge(S["yg_rdy"], b)
                go("yn_rdy", yn[:, :], yv[:, :], ACT.Identity, scale=ga[:, :], bias=gc[:, :])

            def hi_dt(n):
                part_hi(n, "dtv_rdy", "dt_hi", dtv, dt3, "dt_parts_out")

            def hi_u(n):
                part_hi(n, "uv_rdy", "u_hi", uv, u3, "u_parts_out")

            def mid_dt(n):
                part_mid(n, "dt_res", "dt_mid", dtr, dt3)

            def mid_u(n):
                part_mid(n, "u_res", "u_mid", ur, u3)

            def ln_rstd(n):
                tok = slice(n * TT, (n + 1) * TT)
                act.wait_ge(S["ln_mv"], n + 1)
                go("ln1_log", r1[:, tok], mv1[:, tok, 1], ACT.Ln, bias=eps_t[:, :])
                go("ln2_log", r2[:, tok], mv1[:, tok, 1], ACT.Ln, scale=1.0 + EPS, bias=eps2_t[:, :])
                act.wait_ge(S["ln1_log"], n + 1)
                go("ln1_rstd", r1[:, tok], r1[:, tok], ACT.Exp, scale=-0.5)
                act.wait_ge(S["ln2_log"], n + 1)
                go("ln2_rstd", r2[:, tok], r2[:, tok], ACT.Exp, scale=-0.5)

            def sequence(b, before, after):
                n = b + 1
                for g in range(NG):
                    if g < NG - 2 or after:
                        decay(*ahead(b, g, 2))
                    if isfirst(b) and g in (8, 11):
                        ln_rstd({8: 2, 11: 3}[g])
                    if after and g == 0:
                        ln1(n)
                    if before:
                        if g == 0:
                            f_out(b - 1)
                        if g == 2:
                            experts_sigmoid(0, b - 1)
                            experts_sigmoid(1, b - 1)
                            experts_sigmoid(2, b - 1)
                        if g == 6:
                            rstd(b - 1, "gn_var", "gn_log", "gn_rstd", gvar[:, :], gr[:, :])
                        if g == 7:
                            gn_apply(b - 1)
                    if g == 5:
                        z_sigmoid(0, b)
                        z_sigmoid(1, b)
                        z_sigmoid(2, b)
                    if after:
                        if g == 1:
                            ln2(n)
                            xn_out(n)
                        if g == 2:
                            h_out(n)
                        if g == 3:
                            x_out(n)
                            conv_0(n)
                        if g == 4:
                            softplus_sides(n)
                            softplus_exp(n)
                            softplus_log(n)
                        if g == 6:
                            hi_dt(n)
                            conv_sigmoid(0, n)
                            conv_sigmoid(1, n)
                            conv_sigmoid(2, n)
                        if g == 7:
                            rt_exp(n)
                            bc_out(n)
                            state_sigmoid(0, n)
                            mid_dt(n)
                        if g == 8:
                            hi_u(n)
                        if g == 9:
                            mid_u(n)
                        if g == 10:
                            state_sigmoid(1, n)
                            state_sigmoid(2, n)
                        if g == 12:
                            zl_out(n)
                        if g == 13:
                            g_parts_out(n)

            act.preload_act_table_set("natural_log_exp_and_others")
            act.wait_ge(S["vec_in"], 16)
            go("set_act", a_neg[:, :], v(V_A, NG), ACT.Exp)
            act.wait_ge(S["set_act"], 1)
            go("set_act", a_neg[:, :], a_neg[:, :], ACT.Copy, scale=-1.0)
            act.wait_ge(S["set_dve"], 1)
            ln_rstd(0)
            ln1(0)
            h_out(0)
            xn_out(0)
            x_out(0)
            conv_0(0)
            softplus_sides(0)
            softplus_exp(0)
            softplus_log(0)
            conv_sigmoid(0, 0)
            conv_sigmoid(1, 0)
            conv_sigmoid(2, 0)
            rt_exp(0)
            bc_out(0)
            mid_dt(0)
            ln_rstd(1)
            state_sigmoid(0, 0)
            state_sigmoid(1, 0)
            zl_out(0)
            act.wait_ge(S["set_act"], 2)
            decay(0, 0)
            g_parts_out(0)
            decay(0, 1)
            state_sigmoid(2, 0)
            sequence(0, False, True)
            with act.Fori(1, B - 1) as b:
                sequence(b, True, True)
            sequence(B - 1, True, False)
            f_out(B - 1)
            for part in range(3):
                experts_sigmoid(part, B - 1)
            rstd(B - 1, "gn_var", "gn_log", "gn_rstd", gvar[:, :], gr[:, :])

        @block.gpsimd
        def _(pool):
            def tt(name, dst, a, b, op):
                pool.tensor_tensor(dst, a, b, op).then_inc(S[name], 1)

            def outputs(b, g):
                waits = [("scan_done", stepno(b, g))]
                if g == 0:
                    waits.append(("c_row_rdy", 16 * (b + 1)))
                if not (isfirst(b) and g < RING):
                    waits.append(("sums_done", b * NQ + g // NQ - 1))
                wait_apart(pool, *waits)
                tt("hc_rdy", hc[:, g % RING, :], hs[:, g % RING, :], c_row[:, slot(b)], ALU.mult)

            def softplus(n):
                wait_apart(pool, ("sp_pos", n + 1), ("sp_ln", n + 1),
                           *([] if isfirst(n) else [("u_lo", n)]))
                tt("dtv_rdy", dtv[:, :], spp[:, :], sp[:, :], ALU.add)

            def dt_split(n):
                pool.wait_ge(S["dt_hi"], n + 1)
                tt("dt_res", dtr[:, :], dtv[:, :], dt3[:, 0, :], ALU.subtract)

            def u_split(n, k):
                pool.wait_ge(S[("u_hi", "u_mid")[k]], n + 1)
                if k == 0:
                    tt("u_res", ur[:, :], uv[:, :], u3[:, 0, :], ALU.subtract)
                else:
                    tt("u_lo", u3[:, 2, :], ur[:, :], u3[:, 1, :], ALU.subtract)

            def x_silu(n):
                wait_apart(pool, ("sx_rdy", n + 1), ("cv_rdy", n + 1))
                tt("xc_rdy", xc[:, slot(n)], cv1[:, :], sx_t[:, :], ALU.mult)

            def x_dt(n):
                wait_apart(pool, ("xc_rdy", n + 1), ("dtv_rdy", n + 1))
                tt("uv_rdy", uv[:, :], dtv[:, :], xc[:, slot(n)], ALU.mult)

            def z_silu(n):
                wait_apart(pool, ("sz_rdy", n + 1))
                tt("zs_rdy", zs[:, slot(n)], zl[:, :], sz_t[:, :], ALU.mult)

            def f_silu(b):
                pool.wait_ge(S["sf_rdy"], b + 1)
                if not isfirst(b):
                    pool.wait_ge(S["o2_rdy"], b)
                tt("gf_rdy", gf[:, :], fv[:, :], sf_t[:, :], ALU.mult)

            def times_g(b):
                pool.wait_ge(S["o1_rdy"], b + 1)
                pool.wait_ge(S["gf_rdy"], b + 1)
                tt("o2_rdy", o1[:, :], o1[:, :], gf[:, :], ALU.mult)

            def plus_x(b):
                wait_apart(pool, ("o2_rdy", b + 1), ("xch_in", 16),
                           *([] if isfirst(b) else [("out_done", 16 * b)]))
                tt("o3_rdy", o3[:, :], o1[:, :], x_ch[:, cols(b)], ALU.add)

            def sequence(b, before, after):
                n = b + 1
                for g in range(NG):
                    if g < NG - 1 or after:
                        outputs(b, g)
                    if before:
                        if g == 3:
                            f_silu(b - 1)
                        if g == 12:
                            times_g(b - 1)
                        if g == 14:
                            plus_x(b - 1)
                    if g == 5:
                        z_silu(b)
                    if after:
                        if g == 4:
                            softplus(n)
                        if g == 6:
                            dt_split(n)
                            x_silu(n)
                        if g == 7:
                            x_dt(n)
                        if g == 8:
                            u_split(n, 0)
                        if g == 9:
                            u_split(n, 1)

            pool.memset(idle_b, 0.0).then_inc(S["set_pool"], 1)
            dt_split(0)
            sequence(0, False, True)
            with pool.Fori(1, B - 1) as b:
                sequence(b, True, True)
            sequence(B - 1, True, False)
            f_silu(B - 1)
            b = B - 1
            pool.wait_ge(S["gf_rdy"], b + 1)
            pool.wait_ge(S["o3_rdy"], b)
            for half in HALVES:
                tt("gfx_rdy", o1[:, half], xn_ch[:, b * L:][:, half], gf[:, half], ALU.mult)
            for k, half in enumerate(HALVES):
                pool.wait_ge(S["gfx_rdy"], 1 + k)
                tt("rest_rdy", o1[:, half], o1[:, half], x_ch[:, b * L:][:, half], ALU.add)

        @block.tensor
        def _(pe):
            def flip(n, src, rdy, after, done, first=work):
                pe.wait_ge(S[rdy], n + 1)
                after()
                for t in range(TT):
                    mm = pe.transpose(bank(n, first)[:, t * 128:(t + 1) * 128], src[:, t, :], ident)
                mm.then_inc(S[done], 1)

            def project(n, w, after, done, first=work):
                after()
                pe.matmul(bank(n, first)[:, :], win[:, w:w + D], h_ch[:, cols(n)], start=True, stop=True).then_inc(
                    S[done], 1)

            def last(name, count):
                def wait():
                    pe.wait_ge(S[name], count)
                return wait

            def nothing():
                pass

            def scores(n, after):
                after()
                for t in range(TT):
                    mm = pe.matmul(bank(n, s_ps)[:, t * E:(t + 1) * E], xn_now[:, t * 128:(t + 1) * 128],
                                   win[:, W_CEN:W_CEN + E], start=True, stop=True)
                mm.then_inc(S["pe_score"], 1)

            def gate_parts(n, after):
                wait_apart(pe, ("rt_lo", n + 1))
                after()
                for t in range(TT):
                    mm = pe.transpose(work_b[0:SP3 * E, t * 128:(t + 1) * 128],
                                      gate3[:, t, :, :].rearrange("p s e -> p (s e)"), ident_b[:, :])
                mm.then_inc(S["pe_gparts"], 1)

            def spread(b, g, ps, parts, now):
                q, j = divmod(g, NQ)
                if isfirst(b) and g < NQ:
                    for s in range(SP3):
                        mm = pe.matmul(ps, sel_ch[32 * j:32 * j + 32, q, :, :].rearrange("p n i -> p (n i)"),
                                       now[32 * j:32 * j + 32, s, :], start=(s == 0), stop=(s == SP3 - 1))
                    return mm
                return pe.matmul(ps, sel_ch[0:SP3 * 32, q, :, :].rearrange("p n i -> p (n i)"),
                                 parts[:, j, slot(b)], start=True, stop=True)

            def spread_dt(b, g):
                if isfirst(b):
                    if g == 0:
                        pe.wait_ge(S["dt_mid"], 1)
                        pe.wait_ge(S["dt_lo"], 1)
                    if g == NQ:
                        pe.wait_ge(S["dt_parts_rdy"], 16)
                elif g == 0:
                    pe.wait_ge(S["dt_parts_rdy"], 16 * (b + 1))
                if not (isfirst(b) and g < 1):
                    pe.wait_ge(S["da_rdy"], stepno(b, g) - 1)
                spread(b, g, da_ps[:, :], dt_parts, dt3).then_inc(S["dt_bc"], 1)

            def spread_u(b, g):
                if isfirst(b):
                    if g == 0:
                        pe.wait_ge(S["u_mid"], 1)
                        pe.wait_ge(S["u_lo"], 1)
                    if g == NQ:
                        pe.wait_ge(S["u_parts_rdy"], 16)
                elif g == 0:
                    pe.wait_ge(S["u_parts_rdy"], 16 * (b + 1))
                if not (isfirst(b) and g < 2):
                    pe.wait_ge(S["dbu_rdy"], stepno(b, g) - 2)
                spread(b, g, u_ps[g % 2][:, :], u_parts, u3).then_inc(S["u_bc"], 1)

            def spread_gate(b, e):
                wait_apart(pe, *([("g_parts_rdy", b + 1)] if e == 0 else []),
                           *([] if isfirst(b) and e < 1 else [("xg_rdy", stepno(b, e) - 1)]))
                pe.matmul(g_ps[:, :], sel_ex[:, e, :], g_parts[:, slot(b)], start=True, stop=True).then_inc(
                    S["g_bc"], 1)

            def expert(b, e):
                pe.wait_ge(S["xg_rdy"], stepno(b, e))
                mm = pe.matmul(f_ps[:, :], wr[:, e, :], xg[:, e % 2, :], start=False, stop=(e == E - 1))
                mm.then_inc(S["ffn_done"], 1)

            def shared_tokens(b):
                if not isfirst(b):
                    pe.wait_ge(S["fv_rdy"], b)
                pe.matmul(f_ps[:, :], wsum[:, :], xn_ch[:, cols(b)], start=True, stop=False)

            def gated_biases(b):
                if isfirst(b):
                    pe.wait_ge(S["br_lo"], 1)
                for k in range(SP3):
                    pe.matmul(f_ps[:, :], br_parts[:, k, :], g_parts[:, slot(b)], start=False, stop=False)

            def state_mean(b, q):
                pe.wait_ge(S["scan_done"], b * NG + NQ * (q + 1))
                if q == 0 and not isfirst(b):
                    pe.wait_ge(S["sv_rdy"], b)
                for j in range(NQ):
                    tile = slice(32 * j, 32 * j + 32)
                    mm = pe.matmul(s_ps[tile, :], sel_s, hs[:, (NQ * q + j) % RING, :],
                                   start=(q == 0), stop=(q == NQ - 1))
                mm.then_inc(S["means_done"], 1)

            def state_sum(b, q):
                if not isinstance(b, int) or (b, q) != (B - 1, NQ - 1):
                    pe.wait_ge(S["hc_rdy"], b * NG + NQ * (q + 1))
                else:
                    pe.wait_ge(S["hc_rdy"], B * NG - 1)
                    pe.wait_ge(S["last_hc_rdy"], 1)
                if q == 0 and not isfirst(b):
                    pe.wait_ge(S["gn_var"], b)
                for j in range(NQ):
                    tile = slice(32 * j, 32 * j + 32)
                    mm = pe.matmul(y_ps[tile, :], sel_y[:, q, :], hc[:, (NQ * q + j) % RING, :],
                                   start=(q == 0), stop=(q == NQ - 1))
                mm.then_inc(S["sums_done"], 1)

            def gn_mean(b):
                pe.wait_ge(S["gn_mv"], b + 1)
                pe.matmul(y_ps[:, 0:2], g_avg, gmv[:, :], start=True, stop=True).then_inc(S["pe_gmu"], 1)

            def gn_spread(b):
                pe.wait_ge(S["gn_mu"], b + 1)
                pe.wait_ge(S["gn_dm2"], b + 1)
                pe.matmul(y_ps[:, 0:1], g_avg, dm2[:, :], start=True, stop=True).then_inc(S["pe_gvar"], 1)

            def out_res(b, after):
                after()
                if isfirst(b):
                    pe.wait_ge(S["wout_in"], 16)
                pe.matmul(work[:, :], wout[:, O_RES:O_RES + D], h_ch[:, cols(b)], start=True, stop=False)

            def out_s(b):
                pe.wait_ge(S["sv_rdy"], b + 1)
                pe.matmul(work[:, :], wout[:, O_S:O_S + D], sv[:, :], start=False, stop=False)

            def out_y(b):
                pe.wait_ge(S["yg_rdy"], b + 1)
                pe.matmul(work[:, :], wout[:, O_Y:O_Y + D], yg[:, :], start=False, stop=True).then_inc(S["pe_out"], 1)

            def sequence(b, before, after):
                n = b + 1
                for g in range(NG):
                    if g < NG - 2 or after:
                        spread_u(*ahead(b, g, 2))
                    if g < NG - 2 or after:
                        spread_dt(*ahead(b, g, 2))
                    if before and g == 0:
                        expert(b - 1, E - 1)
                    if g == 1:
                        if before:
                            state_sum(b - 1, NQ - 1)
                        if not isfirst(b):
                            shared_tokens(b)
                    if g == 2:
                        gated_biases(b)
                    if g >= 1:
                        expert(b, g - 1)
                    if before and g == 0:
                        state_mean(b - 1, NQ - 1)
                    if g in (5, 8, 13):
                        state_mean(b, (5, 8, 13).index(g))
                    if g in (7, 11, 14):
                        state_sum(b, (7, 11, 14).index(g))
                    if after and g == 1:
                        flip(n, xn_tok, "xn_tok_rdy", last("zl_rdy", 1) if isfirst(b) else last("g_parts_rdy", n),
                             "pe_xn")
                    if after and g == 2:
                        flip(n, xh_tok, "xh_tok_rdy", last("xn_ch_rdy", n + 1), "pe_h")
                    if after and g == 3:
                        project(n, W_X, last("h_ch_rdy", n + 1), "pe_x")
                    if before and g == 4:
                        gn_mean(b - 1)
                    if after and g == 4:
                        project(n, W_DT, last("xpad_rdy", n + 1), "pe_dt")
                    if before and g == 5:
                        gn_spread(b - 1)
                    if after and g == 5:
                        scores(n, last("sp_abs", n + 1))
                    if after and g == 6:
                        project(n, W_SBC, last("rt_sc", n + 1), "pe_sg")
                    if before and g == 8:
                        out_res(b - 1, last("sg_e", n + 1) if after else last("g_parts_rdy", b + 1))
                    if before and g == 9:
                        out_s(b - 1)
                    if before and g == 10:
                        out_y(b - 1)
                    if after and g == 12:
                        project(n, W_Z, last("o1_rdy", b) if before else last("sg_e", n + 1), "pe_z")
                    if after and g == 13:
                        gate_parts(n, last("zl_rdy", n + 1))
                    if g < NG - 1 or after:
                        spread_gate(*ahead(b, g, 1))

            sel_rows = sel_ch[:, :, :, :].rearrange("p q n i -> p (q n i)")

            def keep_clock(matmuls, ps=u_ps[1], values=idle_b):
                for _ in range(matmuls):
                    pe.matmul(ps[:, :], values[:, 0:128], values, start=True, stop=True)

            pe.wait_ge(S["set_pool"], 1)
            keep_clock(12)
            pe.wait_ge(S["cst_in"], 16)
            flip(0, xh_tok, "xh_tok_rdy", nothing, "pe_h", g_ps)
            flip(0, xn_tok, "xn_tok_rdy", nothing, "pe_xn")
            keep_clock(4)
            pe.wait_ge(S["win_in"], 16)
            project(0, W_X, last("h_ch_rdy", 1), "pe_x", u_ps[0])
            project(0, W_DT, nothing, "pe_dt", da_ps)
            keep_clock(2)
            scores(0, last("xn_ch_rdy", 1))
            project(0, W_SBC, nothing, "pe_sg", y_ps)
            pe.wait_ge(S["consts_ready"], 3)
            pe.wait_ge(S["wr_in"], 16)
            shared_tokens(0)
            project(0, W_Z, last("xn_ch_rdy", 1), "pe_z")
            keep_clock(20)
            spread_dt(0, 0)
            keep_clock(3)
            spread_u(0, 0)
            spread_u(0, 1)
            spread_dt(0, 1)
            gate_parts(0, last("zl_rdy", 1))
            keep_clock(4, g_ps)
            spread_gate(0, 0)
            sequence(0, False, True)
            with pe.Fori(1, B - 1) as b:
                sequence(b, True, True)
            sequence(B - 1, True, False)
            state_sum(B - 1, NQ - 1)
            expert(B - 1, E - 1)
            state_mean(B - 1, NQ - 1)
            b = B - 1
            pe.wait_ge(S["o1_rdy"], b)
            pe.wait_ge(S["xg_rdy"], stepno(b, E - 1))
            gn_mean(b)
            for ps, half in zip(LAST_BANKS, HALVES):
                pe.matmul(ps[:, half], wout[:, O_RES:O_RES + D], h_ch[:, b * L:][:, half], start=True, stop=False)
            gn_spread(b)
            pe.wait_ge(S["sv_rdy"], B)
            for ps, half in zip(LAST_BANKS, HALVES):
                pe.matmul(ps[:, half], wout[:, O_S:O_S + D], sv[:, half], start=False, stop=False)
            keep_clock(6, values=sel_rows)
            for k, (ps, half) in enumerate(zip(LAST_BANKS, HALVES)):
                pe.wait_ge(S["yg_rdy"], B + k)
                pe.matmul(ps[:, half], wout[:, O_Y:O_Y + D], yg[:, half], start=False, stop=True).then_inc(
                    S["pe_out"], 1)


def kernel(**inputs):
    import concourse.bacc as bacc
    from concourse.bass_utils import run_bass_kernel_spmd

    a = {k: np.asarray(val) for k, val in inputs.items()}
    x = np.ascontiguousarray(a["L0_attn_u"])

    def f(v):
        return np.asarray(v, np.float32)

    p = np.arange(128)
    const = np.zeros((128, C_END), np.float32)
    const[:, C_ID:C_ID + 128] = np.eye(128)
    const[:, C_AVG:C_AVG + 128] = (p[:, None] // DS == p[None, :] // DS) / (D // GN)
    for q in range(NQ):
        const[p, C_Y + 32 * q + NI * q + p % NI] = 1.0
        for s in range(NQ):
            for i in range(NI):
                const[32 * s + NI * q + i, C_B + NI * q + i] = 1.0
    const[p, C_S + p // NI] = 1.0 / D
    for s in range(SP3):
        const[E * s + np.arange(E), C_G + np.arange(E)] = 1.0

    w = a["L0_attn_in_proj_w"].T
    parts = {name: w[:, lo:hi] for name, lo, hi in (
        ("x", 0, D), ("z", D, 2 * D), ("dt", 2 * D, 3 * D), ("res", 3 * D, 4 * D),
        ("b", 4 * D, 4 * D + DS), ("c", 4 * D + DS, 4 * D + 2 * DS), ("sg", 4 * D + 2 * DS, 4 * D + 3 * DS))}
    sg_tiles = np.zeros((D, NQ, 32), np.float32)
    sg_tiles[:, :, 0:DS] = parts["sg"][:, None, :]
    sg_tiles[:, 0, DS:] = parts["b"]
    sg_tiles[:, 1, DS:] = parts["c"]
    w_in = np.concatenate([parts["dt"], parts["x"], parts["z"], sg_tiles.reshape(D, D), a["L0_ffn_centroids"].T], 1)
    wo = a["L0_attn_out_proj_w"].T
    wos = np.zeros((NQ, 32, D), np.float32)
    wos[:, 0:DS, :] = wo[None, D:D + DS, :]
    w_out = np.concatenate([parts["res"], wo[0:D], wos.reshape(D, D)], 1)
    a_rows = a["L0_attn_A_log"].reshape(NQ, NQ, NI, DS).transpose(3, 2, 1, 0).reshape(128, NG)
    vec = np.concatenate([
        a["L0_attn_conv_w"][:, 0, :], *[a["L0_attn_" + k][:, None] for k in
                                        ("conv_b", "ln_g", "ln_b", "gn_g", "gn_b", "D")],
        a["L0_ffn_bs"].T, a_rows, np.broadcast_to(a["L0_ffn_expert_biases"], (128, E))], 1)
    arrays = {
        "x": x, "xT": x.reshape(B * L, D).T, "const": const, "vec": vec, "w_in": w_in, "w_out": w_out,
        "w_r": a["L0_ffn_Wr"].transpose(2, 0, 1), "w_s": a["L0_ffn_Ws"].transpose(2, 0, 1),
        "b_r": np.tile(a["L0_ffn_br"], (SP3, 1)),
    }
    arrays = {k: np.ascontiguousarray(val) for k, val in arrays.items()}

    nc = bacc.Bacc("TRN2", target_bir_lowering=False, num_devices=1)
    args = [nc.dram_tensor(f"in_{k}", val.shape, mybir.dt.from_np(val.dtype), kind="ExternalInput").ap()
            for k, val in arrays.items()]
    args.append(nc.dram_tensor("out_ch", (D, B * L), F32, kind="ExternalOutput").ap())
    args += [nc.dram_tensor(name, (NQ, SP3 * 32, B * L), BF16, kind="Internal").ap()
             for name in ("dt_moved", "u_moved")]
    mamba_moe(nc, *args)
    r = run_bass_kernel_spmd(nc, [{f"in_{k}": val for k, val in arrays.items()}], core_ids=[0])
    return np.ascontiguousarray(r.results[0]["out_ch"].T.reshape(B, L, D))
```
